# Optimizing a Trainium2 kernel written in Bass

```python
import numpy as np
import jax
import jax.numpy as jnp

def _softmax(x, axis=-1):
    return jax.nn.softmax(x, axis=axis)
def _gelu(x):
    return jax.nn.gelu(x, approximate=True)
def _silu(x):
    return jax.nn.silu(x)
def _sigmoid(x):
    return jax.nn.sigmoid(x)
def _layernorm(x, axis=-1, eps=1e-5):
    m = jnp.mean(x, axis=axis, keepdims=True)
    v = jnp.var(x, axis=axis, keepdims=True)
    return (x - m) / jnp.sqrt(v + eps)
def _scatter_add(tgt, idx, src, axis=0):
    return tgt.at[idx].add(src)
def _segment_sum(src, seg, n):
    return jax.ops.segment_sum(src, seg, n)

kernel_name = 'mk_adj_ffn_d1_adj_256_5c46cc'

def setup_inputs(seed: int = 0):
    np.random.seed(seed)
    _w = jnp.asarray
    def _rec_inputs():
        import jax
        import jax.numpy as jnp
        _gk = jax.random.key(seed)
        x = -0.0002928 + 1 * jax.random.normal(jax.random.fold_in(_gk, 1), (16, 1024, 256), jnp.float32)
        _a = jax.random.bernoulli(jax.random.fold_in(_gk, 2), 0.015625, (16, 1024, 1024))
        _a = jnp.logical_or(_a, jnp.swapaxes(_a, -1, -2))
        _a = jnp.logical_or(_a, jnp.eye(1024, dtype=bool))
        adj = _a.astype(jnp.int32)
        return x, adj
    x, adj = _rec_inputs()
    def _L0_gnn_setup():
        import jax, jax.numpy as jnp
        import numpy as np
        B, N, DIN, DOUT = (16, 1024, 256, 256)
        NEG_SLOPE = 0.2
        key = jax.random.key(seed)
        k1, k2, k3, k4 = jax.random.split(key, 4)
        h = jax.random.normal(k1, (B, N, DIN), dtype=jnp.float32)
        adj_mask = jax.random.randint(k2, (B, N, N), 0, 2, dtype=jnp.int32)
        W = jax.random.normal(k3, (DOUT, DIN), dtype=jnp.float32) * (1.0 / np.sqrt(DIN))
        a = jax.random.normal(k4, (2 * DOUT,), dtype=jnp.float32) * (1.0 / np.sqrt(2 * DOUT))
        return {'h': h, 'adj_mask': adj_mask, 'W': W, 'a': a}
    _L0_gnn_all = _L0_gnn_setup()
    _L0_gnn_in = {k: v for k, v in _L0_gnn_all.items() if k in ('W', 'a', )}
    del _L0_gnn_all

    def _L0_ffn_setup():
        import jax, jax.numpy as jnp
        import numpy as np
        BN_EPS = 0.001

        def _bn(h, g, b, m, v):
            return g * (h - m) * jax.lax.rsqrt(v + BN_EPS) + b
        key = jax.random.key(seed)
        ks = jax.random.split(key, 8)
        B, F, Df = (256, 64, 256)
        E, H, D = (8, 256, 256)
        s1 = 1.0 / np.sqrt(Df)
        s2 = 1.0 / np.sqrt(H)
        return {'x': jax.random.normal(ks[0], (B, F, Df), jnp.float32), 'Wr': jax.random.normal(ks[1], (Df, E), jnp.float32) * s1, 'br': jnp.zeros((E,), jnp.float32), 'W1': jax.random.normal(ks[2], (E, Df, H), jnp.float32) * s1, 'b1': jnp.zeros((E, H), jnp.float32), 'g1': jnp.ones((E, H), jnp.float32), 'be1': jnp.zeros((E, H), jnp.float32), 'm1': jnp.zeros((E, H), jnp.float32), 'v1': jnp.ones((E, H), jnp.float32), 'W2': jax.random.normal(ks[3], (E, H, H), jnp.float32) * s2, 'b2': jnp.zeros((E, H), jnp.float32), 'g2': jnp.ones((E, H), jnp.float32), 'be2': jnp.zeros((E, H), jnp.float32), 'm2': jnp.zeros((E, H), jnp.float32), 'v2': jnp.ones((E, H), jnp.float32), 'Wo': jax.random.normal(ks[4], (E, H, D), jnp.float32) * s2, 'bo': jnp.zeros((E, D), jnp.float32)}
    _L0_ffn_all = _L0_ffn_setup()
    _L0_ffn_in = {k: v for k, v in _L0_ffn_all.items() if k in ('Wr', 'br', 'W1', 'b1', 'g1', 'be1', 'm1', 'v1', 'W2', 'b2', 'g2', 'be2', 'm2', 'v2', 'Wo', 'bo', )}
    del _L0_ffn_all

    return {
        "x": x,
        "adj": adj,
        "L0_gnn_W": _L0_gnn_in["W"],
        "L0_gnn_a": _L0_gnn_in["a"],
        "L0_ffn_Wr": _L0_ffn_in["Wr"],
        "L0_ffn_br": _L0_ffn_in["br"],
        "L0_ffn_W1": _L0_ffn_in["W1"],
        "L0_ffn_b1": _L0_ffn_in["b1"],
        "L0_ffn_g1": _L0_ffn_in["g1"],
        "L0_ffn_be1": _L0_ffn_in["be1"],
        "L0_ffn_m1": _L0_ffn_in["m1"],
        "L0_ffn_v1": _L0_ffn_in["v1"],
        "L0_ffn_W2": _L0_ffn_in["W2"],
        "L0_ffn_b2": _L0_ffn_in["b2"],
        "L0_ffn_g2": _L0_ffn_in["g2"],
        "L0_ffn_be2": _L0_ffn_in["be2"],
        "L0_ffn_m2": _L0_ffn_in["m2"],
        "L0_ffn_v2": _L0_ffn_in["v2"],
        "L0_ffn_Wo": _L0_ffn_in["Wo"],
        "L0_ffn_bo": _L0_ffn_in["bo"],
    }

def reference(x, adj, L0_gnn_W, L0_gnn_a, L0_ffn_Wr, L0_ffn_br, L0_ffn_W1, L0_ffn_b1, L0_ffn_g1, L0_ffn_be1, L0_ffn_m1, L0_ffn_v1, L0_ffn_W2, L0_ffn_b2, L0_ffn_g2, L0_ffn_be2, L0_ffn_m2, L0_ffn_v2, L0_ffn_Wo, L0_ffn_bo):
    import jax
    import jax.numpy as jnp
    def _L0_gnn_ref(h, adj_mask, W, a):
        import jax, jax.numpy as jnp
        import numpy as np
        B, N, DIN, DOUT = (16, 1024, 256, 256)
        NEG_SLOPE = 0.2
        Wh = jnp.einsum('bnd,od->bno', h, W)
        d = Wh.shape[-1]
        a1, a2 = (a[:d], a[d:])
        ei = Wh @ a1
        ej = Wh @ a2
        e = ei[:, :, None] + ej[:, None, :]
        e = jnp.where(e > 0, e, NEG_SLOPE * e)
        e = jnp.where(adj_mask == 0, -jnp.inf, e)
        alpha = jax.nn.softmax(e, axis=-1)
        alpha = jnp.where(jnp.isnan(alpha), 0.0, alpha)
        h_out = jnp.einsum('bij,bjo->bio', alpha, Wh)
        return h_out

    def _L0_ffn_ref(x, Wr, br, W1, b1, g1, be1, m1, v1, W2, b2, g2, be2, m2, v2, Wo, bo):
        import jax, jax.numpy as jnp
        import numpy as np
        BN_EPS = 0.001

        def _bn(h, g, b, m, v):
            return g * (h - m) * jax.lax.rsqrt(v + BN_EPS) + b
        feat = jnp.mean(x, axis=0)
        w = jax.nn.softmax(feat @ Wr + br, axis=-1)
        h = jnp.einsum('bfd,edh->bfeh', x, W1) + b1
        h = jax.nn.relu(_bn(h, g1, be1, m1, v1))
        h = jnp.einsum('bfeh,ehk->bfek', h, W2) + b2
        h = jax.nn.relu(_bn(h, g2, be2, m2, v2))
        y = jnp.einsum('bfeh,ehd->bfed', h, Wo) + bo
        return jnp.einsum('bfed,fe->bfd', y, w)

    x = x + _L0_gnn_ref(_layernorm(x, axis=-1), adj, L0_gnn_W, L0_gnn_a)
    x = x + _L0_ffn_ref(_layernorm(x, axis=-1), L0_ffn_Wr, L0_ffn_br, L0_ffn_W1, L0_ffn_b1, L0_ffn_g1, L0_ffn_be1, L0_ffn_m1, L0_ffn_v1, L0_ffn_W2, L0_ffn_b2, L0_ffn_g2, L0_ffn_be2, L0_ffn_m2, L0_ffn_v2, L0_ffn_Wo, L0_ffn_bo)
    return x


_drawn_inputs = setup_inputs


def setup_inputs(seed=0):
    import zlib

    import numpy as np

    out = dict(_drawn_inputs(seed))
    spreads = {'L0_ffn_br': (0.0, 0.1),
     'L0_ffn_b1': (0.0, 0.43),
     'L0_ffn_g1': (1.0, 0.2),
     'L0_ffn_be1': (0.0, 0.44),
     'L0_ffn_m1': (0.0, 0.424),
     'L0_ffn_v1': (1.0, 0.6),
     'L0_ffn_b2': (0.0, 0.308),
     'L0_ffn_g2': (1.0, 0.2),
     'L0_ffn_be2': (0.0, 0.312),
     'L0_ffn_m2': (0.0, 0.315),
     'L0_ffn_v2': (1.0, 0.6),
     'L0_ffn_bo': (0.0, 0.1)}
    factors = {}
    for name, (base, spread) in spreads.items():
        noise = np.random.default_rng([zlib.crc32(name.encode()), seed]).standard_normal(out[name].shape)
        drawn = base * np.exp(spread * noise) if base else spread * noise
        out[name] = jnp.asarray(drawn.astype(out[name].dtype))
    for name, factor in factors.items():
        out[name] = (out[name] * factor).astype(out[name].dtype)
    return out
```

```python
from contextlib import ExitStack

import concourse.bass as bass
import concourse.mybir as mybir

FP32 = mybir.dt.float32
FP32R = mybir.dt.float32r
BF16 = mybir.dt.bfloat16
INT32 = mybir.dt.int32
ALU = mybir.AluOpType
ACT = mybir.ActivationFunctionType
AX = mybir.AxisListType

P = 128
BANK = 512
LN_EPS = 1e-5
BN_EPS = 1e-3
SLOPE = 0.2
NO_EDGE = -1e30
TINY = 1e-30
DMA = 16


def wait(eng, sem, value):
    if isinstance(value, int) and value <= 0:
        return
    eng.wait_ge(sem, value)


def bits(ap):
    return ap.bitcast(FP32)


def split_matmul(pe, out, w_hi, w_lo, x_hi, x_lo, first, last):
    pe.matmul(out, w_hi, x_hi, start=first, stop=False)
    pe.matmul(out, w_hi, x_lo, start=False, stop=False)
    return pe.matmul(out, w_lo, x_hi, start=False, stop=last)


def program(nc, x, adj, W, a, Wr, br, W1, b1, g1, be1, m1, v1, W2, b2, g2, be2, m2, v2, Wo, bo, out):
    B, N, D = x.shape
    E = Wr.shape[1]
    KB = D // P
    TB = N // P
    PAIRS = B // 2
    UT = 2 * TB
    CT = BANK // P
    CH = N // BANK
    US = CH * E
    DX = D + 2
    assert B % 2 == 0 and D == 2 * P and CH == 2 and E == 8 and TB == 8

    x1_dram = nc.dram_tensor("x1_scratch", [CH, B, P, CT, D], FP32, kind="Internal").ap()

    persistent = ExitStack()
    with persistent:
        def keep(name, shape, dt=FP32):
            return persistent.enter_context(nc.sbuf_tensor(name, shape, dt))

        ident = keep("ident", [P, P])
        minus_half, ln_eps = keep("minus_half", [P, CT]), keep("ln_eps", [P, CT])
        w12_hi = keep("w12_hi", [P, 2, E, KB * D], FP32R)
        w12_lo = keep("w12_lo", [P, 2, E, KB * D], FP32R)
        node_table = keep("node_table", [P, TB, D])
        wr_sb = keep("wr_sb", [P, KB, E])
        br_sb = keep("br_sb", [P, E])
        bo_sb = keep("bo_sb", [E, D])
        bn_rows = [keep(f"bn_rows{i}", [5 * E * KB, P]) for i in range(2)]

        attention_block(nc, x, adj, W, a, W1, W2, x1_dram, ident, minus_half, ln_eps, w12_hi, w12_lo, node_table,
                        (Wr, br, bo, (b1, g1, be1, m1, v1), (b2, g2, be2, m2, v2)),
                        (wr_sb, br_sb, bo_sb, bn_rows))

        w_bc = keep("w_bc", [P, CH, E, BANK])
        wo_hi = keep("wo_hi", [P, E, KB * D], FP32R)
        wo_lo = keep("wo_lo", [P, E, KB * D], FP32R)
        bn_scale = [keep(f"bn_scale{i}", [P, E * KB]) for i in range(2)]
        bn_shift = [keep(f"bn_shift{i}", [P, E * KB]) for i in range(2)]
        gate_block(nc, B, Wo, ident, minus_half, node_table, wr_sb, br_sb, bo_sb, bn_rows,
                   w_bc, wo_hi, wo_lo, bn_scale, bn_shift)
        ffn_block(nc, B, x1_dram, out, ident, minus_half, ln_eps, node_table, w12_hi, w12_lo, wo_hi, wo_lo,
                  w_bc, bn_scale, bn_shift)


def attention_block(nc, x, adj, W, a, W1, W2, x1_dram, ident, minus_half, ln_eps, w12_hi, w12_lo, feat_sum,
                    small_dram, small_sb):
    B, N, D = x.shape
    E = W1.shape[0]
    KB, TB, PAIRS = D // P, N // P, B // 2
    UT, CT = 2 * TB, BANK // P
    DX = D + 2
    HEADS = TB // 2
    Wr, br, bo, bn1, bn2 = small_dram
    wr_sb, br_sb, bo_sb, bn_rows = small_sb
    assert 2 * E == UT

    ctx = ExitStack()
    with ctx:
        def sb(name, shape, dt=FP32):
            return ctx.enter_context(nc.sbuf_tensor(name, shape, dt))

        def ps(name, shape, dt=FP32):
            return ctx.enter_context(nc.psum_tensor(name, shape, dt))

        def sem(name):
            return ctx.enter_context(nc.semaphore(name))

        w_sb = sb("w_sb", [P, KB, D])
        a_sb = sb("a_sb", [P, KB, 2])
        wx_hi, wx_lo = sb("wx_hi", [P, KB, DX], FP32R), sb("wx_lo", [P, KB, DX], FP32R)
        x_sb = [sb(f"x_sb{i}", [P, TB, D]) for i in range(2)]
        adj_sb = [sb(f"adj_sb{i}", [P, N], INT32) for i in range(2)]
        penalty = [sb(f"penalty{i}", [P, N], BF16) for i in range(2)]
        ej_rows = [sb(f"ej_rows{i}", [P, N]) for i in range(2)]
        scores = [sb(f"scores{i}", [P, N]) for i in range(4)]
        scaled = sb("scaled", [P, N])
        pT_hi = [sb(f"pT_hi{i}", [P, TB, P], FP32R) for i in range(2)]
        pT_lo = [sb(f"pT_lo{i}", [P, TB, P], FP32R) for i in range(2)]
        wh_hi = [sb(f"wh_hi{i}", [P, TB, D], FP32R) for i in range(2)]
        wh_lo = [sb(f"wh_lo{i}", [P, TB, D], FP32R) for i in range(2)]
        e_cols = [sb(f"e_cols{i}", [P, TB, 3]) for i in range(2)]
        row_max, shifted, neg_max = (sb(n, [P, 4]) for n in ("row_max", "shifted", "neg_max"))
        row_sum, row_den, row_inv = (sb(n, [P, 4]) for n in ("row_sum", "row_den", "row_inv"))
        x1_sb = [sb(f"x1_sb{i}", [P, D]) for i in range(4)]
        x1_stats, x1_mv = sb("x1_stats", [P, 2, 6]), sb("x1_mv", [P, 4, 2])
        x1_vareps, x1_rstd = sb("x1_vareps", [P, 4]), sb("x1_rstd", [P, 4])
        n1_sb = [sb(f"n1_sb{i}", [P, D]) for i in range(2)]
        xs_stats, xs_mv = sb("xs_stats", [P, 2, 6]), sb("xs_mv", [P, 2, 2, 2])
        xs_vareps, xs_rstd = sb("xs_vareps", [P, 2, 2]), sb("xs_rstd", [P, 2, 2])
        xn_sb = sb("xn_sb", [P, 2, D])
        hT_hi, hT_lo = sb("hT_hi", [P, KB, 2 * P], FP32R), sb("hT_lo", [P, KB, 2 * P], FP32R)
        w_stage = [sb(f"w_stage{i}", [P, KB * D]) for i in range(2)]

        pT_ps = [ps(f"pT_ps{i}", [P, TB, P]) for i in range(2)]
        attn_ps = [ps(f"attn_ps{i}", [P, BANK]) for i in range(2)]
        head_ps = ps("head_ps", [P, 2, BANK])

        small_in = sem("small_in")
        w_in = sem("w_in")
        x_in = [[sem(f"x_in{i}{h}") for h in range(2)] for i in range(2)]
        adj_in = [sem(f"adj_in{i}") for i in range(2)]
        stage_in = [sem(f"stage_in{i}") for i in range(2)]
        x1_stored = [sem(f"x1_stored{i}") for i in range(4)]
        names = """const_zero const_ready wT_ready wx_hi_ready wx_ready
            xs_stat xs_mv_ready xs_vareps_ready xs_rstd_ready xn_ready hT_ready hT_hi_ready hT_lo_ready
            wh_ready wh_hi_ready wh_lo_ready ej_rows_psum ej_rows_ready
            penalty_ready rowmax_ready scaled_ready shifted_ready negmax_ready lrelu_ready probs_ready
            pT_ready pT_hi_ready pT_lo_ready attn_ready den_ready inv_ready x1_ready
            x1_stat x1_mv_ready x1_vareps_ready x1_rstd_ready n1_ready n1_added
            w12_hi_ready w12_lo_ready""".split()
        S = {n: sem(n) for n in names}

        def tile_at(k, u, off, last):
            t = u + off
            ok = (t >= 0 or not isinstance(k, int)) and (t < UT or not last)
            return ok, t, k * UT + (t + 1)

        def head_at(k, u, last):
            g = u + 2
            if g < 0:
                return None
            off = g // TB + 1
            return None if last and off >= 2 else (off, g % TB)

        def parity(t):
            return (t // TB) % 2

        block = ctx.enter_context(nc.Block())

        @block.sync
        def _(sp):
            sp.dma_start(w_sb[:, :, :], W.rearrange("(o p) d -> p o d", p=P)).then_inc(w_in, DMA)
            for h in range(2):
                sp.dma_start(a_sb[:, :, h], a.rearrange("(h o p) -> h p o", p=P, o=KB)[h],
                             allow_slow_non_contiguous=True).then_inc(w_in, DMA)

            def load_x(b, i, half):
                h = slice(half * TB // 2, (half + 1) * TB // 2)
                sp.dma_start(x_sb[i][:, h, :], x[b].rearrange("(t p) d -> p t d", p=P)[:, h, :]) \
                    .then_inc(x_in[i][half], DMA)

            def load_adj(b, it, i):
                sp.dma_start(adj_sb[i][:, :], adj[b, it * P:(it + 1) * P, :]).then_inc(adj_in[i], DMA)

            for half in range(2):
                load_x(0, 0, half)
            load_adj(0, 0, 0)
            load_adj(0, 1, 1)
            for half in range(2):
                load_x(1, 1, half)
            sp.dma_start(wr_sb[:, :, :], Wr.rearrange("(k p) e -> p k e", p=P),
                         allow_slow_non_contiguous=True).then_inc(small_in, DMA)
            sp.dma_start(br_sb[:, :], br.partition_broadcast(P)).then_inc(small_in, DMA)
            sp.dma_start(bo_sb[:, :], bo[:, :]).then_inc(small_in, DMA)
            for rows, params in zip(bn_rows, (bn1, bn2)):
                for i, p in enumerate(params):
                    sp.dma_start(rows[i * E * KB:(i + 1) * E * KB, :],
                                 p.rearrange("e (k p) -> (e k) p", p=P)).then_inc(small_in, DMA)

            def slot(k, u, last):
                ok, t, n = tile_at(k, u, 7, last)
                if ok:
                    wait(sp, S["penalty_ready"], n - 2)
                    load_adj(2 * k + t // TB, t % TB, t % 2)
                ok, t, n = tile_at(k, u, 0, last)
                if ok and t >= 0:
                    wait(sp, S["x1_ready"], n)
                    it = t % TB
                    sp.dma_start(x1_dram[it // CT, 2 * k + t // TB, :, it % CT, :],
                                 x1_sb[t % 4][:, :]).then_inc(x1_stored[t % 4], DMA)
                    if not last and it % CT == CT - 1:
                        load_x(2 * k + t // TB + 2, t // TB, it // CT)

            for u in range(-5, 0):
                slot(0, u, PAIRS == 1)
            if PAIRS > 1:
                with sp.Fori(0, PAIRS - 1) as k:
                    for u in range(UT):
                        slot(k, u, False)
            for u in range(UT):
                slot(PAIRS - 1, u, True)
            for i in range(4):
                sp.wait_ge(x1_stored[i], DMA * (1 + PAIRS * UT // 4))
            sp.wait_ge(small_in, DMA * 13)

        @block.gpsimd
        def _(pool):
            for i in range(4):
                pool.sem_inc(x1_stored[i], DMA)
            pool.sem_inc(S["n1_added"], 2)
            pool.memset(ident[:, :], 0.0).then_inc(S["const_zero"], 1)
            pool.memset(minus_half[:, :], -0.5)
            pool.memset(ln_eps[:, :], LN_EPS)
            pool.memset(feat_sum[:, :, :], 0.0)
            pool.wait_ge(S["const_zero"], 1)
            pool.affine_select(out=ident[:, :], in_=ident[:, :], compare_op=ALU.not_equal, fill=1.0, base=0,
                               pattern=[[-1, P]], channel_multiplier=1).then_inc(S["const_ready"], 1)

            def head_rstd(c, step):
                i = step % 2
                pool.wait_ge(S["xs_mv_ready"], c)
                pool.tensor_tensor(xs_vareps[:, i, :], xs_mv[:, i, :, 1], ln_eps[:, 0:2], ALU.add) \
                    .then_inc(S["xs_vareps_ready"], 1)
                pool.wait_ge(S["xs_vareps_ready"], c)
                pool.tensor_tensor(xs_rstd[:, i, :], xs_vareps[:, i, :], minus_half[:, 0:2], ALU.pow) \
                    .then_inc(S["xs_rstd_ready"], 1)

            def load_weights(task):
                layer, e = task // E, task % E
                pool.dma_start(w_stage[task % 2][:, :].rearrange("p (k d) -> p k d", k=KB),
                               (W1, W2)[layer][e].rearrange("(k p) d -> p k d", p=P)).then_inc(stage_in[task % 2], DMA)

            def split_weights(task):
                layer, e, stage = task // E, task % E, w_stage[task % 2]
                pool.wait_ge(stage_in[task % 2], DMA * (task // 2 + 1))
                pool.tensor_copy(w12_hi[:, layer, e, :], stage[:, :]).then_inc(S["w12_hi_ready"], 1)
                pool.wait_ge(S["w12_hi_ready"], task + 1)
                pool.tensor_tensor(w12_lo[:, layer, e, :], stage[:, :], bits(w12_hi[:, layer, e, :]),
                                   ALU.subtract).then_inc(S["w12_lo_ready"], 1)
                if task + 2 < UT:
                    pool.wait_ge(S["w12_lo_ready"], task + 1)
                    load_weights(task + 2)

            def slot(k, u, last):
                ok, t, n = tile_at(k, u, 1, last)
                if ok:
                    pool.wait_ge(S["x1_mv_ready"], n)
                    pool.tensor_tensor(x1_vareps[:, t % 4:t % 4 + 1], x1_mv[:, t % 4, 1:2], ln_eps[:, 0:1], ALU.add) \
                        .then_inc(S["x1_vareps_ready"], 1)
                    pool.wait_ge(S["x1_vareps_ready"], n)
                    pool.tensor_tensor(x1_rstd[:, t % 4:t % 4 + 1], x1_vareps[:, t % 4:t % 4 + 1],
                                       minus_half[:, 0:1], ALU.pow).then_inc(S["x1_rstd_ready"], 1)
                head = head_at(k, u, last)
                if head and head[1] < HEADS:
                    head_rstd((2 * k + head[0]) * HEADS + (head[1] + 1), head[1])
                ok, t, n = tile_at(k, u, 0, last)
                if ok and t >= 0:
                    pool.wait_ge(S["n1_ready"], n)
                    rows = feat_sum[:, t % TB, :]
                    pool.tensor_tensor(rows, rows, n1_sb[t % 2][:, :], ALU.add).then_inc(S["n1_added"], 1)
                if last and u >= 0:
                    split_weights(u)

            for task in range(2):
                load_weights(task)
            for j in range(HEADS):
                head_rstd(j + 1, j)
            for u in range(-5, 0):
                slot(0, u, PAIRS == 1)
            if PAIRS > 1:
                with pool.Fori(0, PAIRS - 1) as k:
                    for u in range(UT):
                        slot(k, u, False)
            for u in range(UT):
                slot(PAIRS - 1, u, True)

        @block.tensor
        def _(pe):
            pe.wait_ge(S["const_ready"], 1)
            pe.wait_ge(w_in, 3 * DMA)
            for d in range(KB):
                for o in range(KB):
                    pe.transpose(head_ps[:, d, o * P:(o + 1) * P], w_sb[:, o, d * P:(d + 1) * P], ident[:, :])
                for o in range(KB):
                    last = pe.matmul(head_ps[:, d, D:DX], w_sb[:, o, d * P:(d + 1) * P], a_sb[:, o, :],
                                     start=(o == 0), stop=(o == KB - 1))
            last.then_inc(S["wT_ready"], 1)
            pe.wait_ge(S["wx_ready"], 1)

            def head_transpose(b, j):
                if j == 0:
                    wait(pe, S["ej_rows_ready"], b)
                else:
                    pe.wait_ge(S["wh_lo_ready"], b * TB + 2 * j)
                pe.wait_ge(S["xn_ready"], b * HEADS + (j + 1))
                for c in range(2):
                    for d in range(KB):
                        at = d * 2 * P + c * P
                        last = pe.transpose(head_ps[:, 0, at:at + P], xn_sb[:, c, d * P:(d + 1) * P], ident[:, :])
                last.then_inc(S["hT_ready"], 1)

            def head_project(b, j):
                pe.wait_ge(S["hT_lo_ready"], b * HEADS + (j + 1))
                for c in range(2):
                    for d in range(KB):
                        cols = slice(c * P, (c + 1) * P)
                        last = split_matmul(pe, head_ps[:, 1 - c, 0:DX], hT_hi[:, d, cols], hT_lo[:, d, cols],
                                            wx_hi[:, d, :], wx_lo[:, d, :], d == 0, d == KB - 1)
                    last.then_inc(S["wh_ready"], 1)

            def spread_ej(b, i):
                pe.wait_ge(S["wh_lo_ready"], b * TB + TB)
                for t in range(TB):
                    at = (t % CT) * P
                    last = pe.transpose(head_ps[:, t // CT, at:at + P],
                                        e_cols[i][:, t, 1:2].to_broadcast([P, P]), ident[:, :])
                last.then_inc(S["ej_rows_psum"], 1)

            def slot(k, u, last_pair):
                head = head_at(k, u, last_pair)
                if head and head[1] == HEADS + 1:
                    spread_ej(2 * k + head[0], head[0] % 2)
                ok, t, n = tile_at(k, u, 3, last_pair)
                if ok:
                    pe.wait_ge(S["probs_ready"], n)
                    wait(pe, S["pT_lo_ready"], n - 2)
                    for j in range(TB):
                        last = pe.transpose(pT_ps[t % 2][:, j, :], scores[t % 4][:, j * P:(j + 1) * P], ident[:, :])
                    last.then_inc(S["pT_ready"], 1)
                if head and 1 <= head[1] <= HEADS:
                    head_transpose(2 * k + head[0], head[1] - 1)
                ok, t, n = tile_at(k, u, 2, last_pair)
                if ok:
                    pe.wait_ge(S["pT_lo_ready"], n)
                    wait(pe, S["x1_ready"], n - 2)
                    i, acc = parity(t), attn_ps[t % 2][:, 0:D]
                    for j in range(TB):
                        last = split_matmul(pe, acc, pT_hi[t % 2][:, j, :], pT_lo[t % 2][:, j, :],
                                            wh_hi[i][:, j, :], wh_lo[i][:, j, :], j == 0, j == TB - 1)
                    last.then_inc(S["attn_ready"], 1)
                if head and 1 <= head[1] <= HEADS:
                    head_project(2 * k + head[0], head[1] - 1)

            for j in range(HEADS):
                head_transpose(0, j)
                head_project(0, j)
            spread_ej(0, 0)
            for u in range(-5, 0):
                slot(0, u, PAIRS == 1)
            if PAIRS > 1:
                with pe.Fori(0, PAIRS - 1) as k:
                    for u in range(UT):
                        slot(k, u, False)
            for u in range(UT):
                slot(PAIRS - 1, u, True)

        @block.scalar
        def _(act):
            act.wait_ge(S["wT_ready"], 1)
            act.activation(wx_hi[:, :, :], head_ps[:, :, 0:DX], ACT.Copy).then_inc(S["wx_hi_ready"], 1)

            def head_hT(b, j):
                act.wait_ge(S["hT_ready"], b * HEADS + (j + 1))
                act.activation(hT_hi[:, :, :].rearrange("p k c -> p (k c)"), head_ps[:, 0, :], ACT.Copy) \
                    .then_inc(S["hT_hi_ready"], 1)

            def head_wh(b, j, i):
                for c in range(2):
                    t = 2 * j + c
                    act.wait_ge(S["wh_ready"], b * TB + (t + 1))
                    act.activation(wh_hi[i][:, t, :], head_ps[:, 1 - c, 0:D], ACT.Copy) \
                        .then_inc(S["wh_hi_ready"], 1)

            def head_ej(b, i):
                act.wait_ge(S["ej_rows_psum"], b + 1)
                act.activation(ej_rows[i][:, :], head_ps[:, :, :].rearrange("p k c -> p (k c)"), ACT.Copy) \
                    .then_inc(S["ej_rows_ready"], 1)

            def slot(k, u, last):
                head = head_at(k, u, last)
                ok, t, n = tile_at(k, u, 3, last)
                if ok:
                    act.wait_ge(S["pT_ready"], n)
                    wait(act, S["attn_ready"], n - 2)
                    act.activation(pT_hi[t % 2][:, :, :], pT_ps[t % 2][:, :, :], ACT.Copy) \
                        .then_inc(S["pT_hi_ready"], 1)
                if head and 1 <= head[1] <= HEADS:
                    head_hT(2 * k + head[0], head[1] - 1)
                if head and head[1] == HEADS + 1:
                    head_ej(2 * k + head[0], head[0] % 2)
                ok, t, n = tile_at(k, u, 4, last)
                if ok:
                    s, c = scores[t % 4], t % 4
                    act.wait_ge(S["lrelu_ready"], n)
                    act.activation(s[:, :], s[:, :], ACT.Exp, bias=neg_max[:, c:c + 1],
                                   accum_out=row_sum[:, c:c + 1]).then_inc(S["probs_ready"], 1)
                ok, t, n = tile_at(k, u, 5, last)
                if ok:
                    act.wait_ge(S["rowmax_ready"], n)
                    act.activation(scaled[:, :], scores[t % 4][:, :], ACT.Identity, scale=SLOPE,
                                   bias=e_cols[parity(t)][:, t % TB, 2:3]).then_inc(S["scaled_ready"], 1)
                if head and 1 <= head[1] <= HEADS:
                    head_wh(2 * k + head[0], head[1] - 1, head[0] % 2)

            for j in range(HEADS):
                head_hT(0, j)
                head_wh(0, j, 0)
            head_ej(0, 0)
            for u in range(-5, 0):
                slot(0, u, PAIRS == 1)
            if PAIRS > 1:
                with act.Fori(0, PAIRS - 1) as k:
                    for u in range(UT):
                        slot(k, u, False)
            for u in range(UT):
                slot(PAIRS - 1, u, True)

        @block.vector
        def _(dve):
            dve.wait_ge(S["wx_hi_ready"], 1)
            dve.tensor_tensor(wx_lo[:, :, :], head_ps[:, :, 0:DX], bits(wx_hi[:, :, :]), ALU.subtract) \
                .then_inc(S["wx_ready"], 1)

            def head_stats(b, j, i, turn):
                if j % 2 == 0:
                    dve.wait_ge(x_in[i][j // 2], DMA * turn)
                n = b * HEADS + j
                for c in range(2):
                    dve.bn_stats(xs_stats[:, c, :], x_sb[i][:, 2 * j + c, :]).then_inc(S["xs_stat"], 1)

            def head_mean_var(b, j, waited):
                if not waited:
                    dve.wait_ge(S["xs_stat"], 2 * (b * HEADS + (j + 1)))
                for c in range(2):
                    last = dve.bn_aggr(xs_mv[:, j % 2, c, :], xs_stats[:, c, :])
                last.then_inc(S["xs_mv_ready"], 1)

            def head_normalise(b, j, i):
                dve.wait_ge(S["xs_rstd_ready"], b * HEADS + (j + 1))
                wait(dve, S["hT_ready"], b * HEADS + j)
                for c in range(2):
                    last = dve.tensor_scalar(xn_sb[:, c, :], x_sb[i][:, 2 * j + c, :], xs_mv[:, j % 2, c, 0:1],
                                             xs_rstd[:, j % 2, c:c + 1], ALU.subtract, ALU.mult)
                last.then_inc(S["xn_ready"], 1)

            def head_hT(b, j):
                dve.wait_ge(S["hT_hi_ready"], b * HEADS + (j + 1))
                dve.tensor_tensor(hT_lo[:, :, :].rearrange("p k c -> p (k c)"), head_ps[:, 0, :],
                                  bits(hT_hi[:, :, :]).rearrange("p k c -> p (k c)"), ALU.subtract) \
                    .then_inc(S["hT_lo_ready"], 1)

            def head_wh(b, j, i):
                for c in range(2):
                    t = 2 * j + c
                    dve.wait_ge(S["wh_hi_ready"], b * TB + (t + 1))
                    dve.tensor_copy(e_cols[i][:, t, 0:2], head_ps[:, 1 - c, D:DX])
                    dve.tensor_scalar(e_cols[i][:, t, 2:3], head_ps[:, 1 - c, D:D + 1], SLOPE, None, ALU.mult)
                    dve.tensor_tensor(wh_lo[i][:, t, :], head_ps[:, 1 - c, 0:D], bits(wh_hi[i][:, t, :]),
                                      ALU.subtract).then_inc(S["wh_lo_ready"], 1)

            def scores_operands(k, t, n):
                if t % TB == 0:
                    dve.wait_ge(S["ej_rows_ready"], 2 * k + (t // TB + 1))
                wait(dve, S["pT_ready"], n - 4)
                dve.wait_ge(S["penalty_ready"], n)

            def slot(k, u, last):
                head = head_at(k, u, last)
                step = head[1] if head else None
                hb, hi = (2 * k + head[0], head[0] % 2) if head else (None, None)
                post, pt, pn = tile_at(k, u, 1, last)
                new, st, sn = tile_at(k, u, 5, last)
                pc, sc = pt % 4, st % 4
                ok, t, n = tile_at(k, u, 4, last)
                if ok:
                    s = scores[t % 4]
                    dve.wait_ge(S["negmax_ready"], n)
                    dve.wait_ge(S["scaled_ready"], n)
                    dve.scalar_tensor_tensor(s[:, :], s[:, :], e_cols[parity(t)][:, t % TB, 0:1], scaled[:, :],
                                             ALU.add, ALU.max).then_inc(S["lrelu_ready"], 1)
                if post:
                    dve.wait_ge(S["probs_ready"], pn)
                    dve.tensor_scalar(row_den[:, pc:pc + 1], row_sum[:, pc:pc + 1], TINY, None, ALU.max) \
                        .then_inc(S["den_ready"], 1)
                ok, t, n = tile_at(k, u, 3, last)
                if ok:
                    dve.wait_ge(S["pT_hi_ready"], n)
                    wait(dve, S["attn_ready"], n - 2)
                    dve.tensor_tensor(pT_lo[t % 2][:, :, :], pT_ps[t % 2][:, :, :], bits(pT_hi[t % 2][:, :, :]),
                                      ALU.subtract).then_inc(S["pT_lo_ready"], 1)
                if post:
                    dve.wait_ge(S["den_ready"], pn)
                    dve.reciprocal(row_inv[:, pc:pc + 1], row_den[:, pc:pc + 1]).then_inc(S["inv_ready"], 1)
                if new:
                    dve.wait_ge(adj_in[st % 2], DMA * (k * (UT // 2) + (st // 2 + 1)))
                    dve.tensor_scalar(penalty[st % 2][:, :], adj_sb[st % 2][:, :], 0.0, NO_EDGE,
                                      ALU.is_equal, ALU.mult).then_inc(S["penalty_ready"], 1)
                if post:
                    dve.wait_ge(S["inv_ready"], pn)
                    dve.wait_ge(S["attn_ready"], pn)
                    dve.wait_ge(x1_stored[pc], DMA * (k * (UT // 4) + (pt // 4 + 1)))
                    if new:
                        scores_operands(k, st, sn)
                    dve.scalar_tensor_tensor(x1_sb[pc][:, :], attn_ps[pt % 2][:, 0:D], row_inv[:, pc:pc + 1],
                                             x_sb[parity(pt)][:, pt % TB, :], ALU.mult, ALU.add) \
                        .then_inc(S["x1_ready"], 1)
                if new:
                    if not post:
                        scores_operands(k, st, sn)
                    dve.tensor_tensor_reduce(out=scores[sc][:, :], in0=penalty[st % 2][:, :],
                                             in1=ej_rows[parity(st)][:, :], scale=1.0, scalar=NO_EDGE / 2,
                                             op0=ALU.add, op1=ALU.max, accum_out=row_max[:, sc:sc + 1]) \
                        .then_inc(S["rowmax_ready"], 1)
                if post:
                    dve.wait_ge(S["x1_ready"], pn)
                    dve.bn_stats(x1_stats[:, pt % 2, :], x1_sb[pc][:, :]).then_inc(S["x1_stat"], 1)
                if new:
                    if post:
                        dve.wait_ge(S["x1_stat"], pn)
                    dve.wait_ge(S["rowmax_ready"], sn)
                    dve.tensor_scalar(shifted[:, sc:sc + 1], row_max[:, sc:sc + 1], -1.0,
                                      e_cols[parity(st)][:, st % TB, 0:1], ALU.mult, ALU.subtract) \
                        .then_inc(S["shifted_ready"], 1)
                if post:
                    if not new:
                        dve.wait_ge(S["x1_stat"], pn)
                    dve.bn_aggr(x1_mv[:, pc, :], x1_stats[:, pt % 2, :]).then_inc(S["x1_mv_ready"], 1)
                if new:
                    dve.wait_ge(S["shifted_ready"], sn)
                    dve.scalar_tensor_tensor(neg_max[:, sc:sc + 1], shifted[:, sc:sc + 1], SLOPE,
                                             shifted[:, sc:sc + 1], ALU.mult, ALU.min) \
                        .then_inc(S["negmax_ready"], 1)
                if head and 1 <= step <= HEADS:
                    head_hT(hb, step - 1)
                if head and step < HEADS:
                    head_stats(hb, step, hi, k + (head[0] // 2 + 1))
                ok, t, n = tile_at(k, u, 0, last)
                if ok and t >= 0:
                    dve.wait_ge(S["x1_rstd_ready"], n)
                    dve.wait_ge(S["n1_added"], n)
                    if head and step < HEADS:
                        dve.wait_ge(S["xs_stat"], 2 * (hb * HEADS + (step + 1)))
                    dve.tensor_scalar(n1_sb[t % 2][:, :], x1_sb[t % 4][:, :], x1_mv[:, t % 4, 0:1],
                                      x1_rstd[:, t % 4:t % 4 + 1], ALU.subtract, ALU.mult) \
                        .then_inc(S["n1_ready"], 1)
                if head and step < HEADS:
                    head_mean_var(hb, step, ok and t >= 0)
                if head and 1 <= step <= HEADS:
                    head_wh(hb, step - 1, hi)
                if head and step < HEADS:
                    head_normalise(hb, step, hi)

            for j in range(HEADS):
                head_stats(0, j, 0, 1)
                head_mean_var(0, j, False)
                head_normalise(0, j, 0)
                head_hT(0, j)
                head_wh(0, j, 0)
            for u in range(-5, 0):
                slot(0, u, PAIRS == 1)
            if PAIRS > 1:
                with dve.Fori(0, PAIRS - 1) as k:
                    for u in range(UT):
                        slot(k, u, False)
            for u in range(UT):
                slot(PAIRS - 1, u, True)


def gate_block(nc, B, Wo, ident, minus_half, node_table, wr_sb, br_sb, bo_sb, bn_rows, w_bc, wo_hi, wo_lo,
               bn_scale, bn_shift):
    TB, D = node_table.shape[1], node_table.shape[2]
    E, KB = wr_sb.shape[2], D // P
    CT = BANK // P
    EK = E * KB

    ctx = ExitStack()
    with ctx:
        def sb(name, shape, dt=FP32):
            return ctx.enter_context(nc.sbuf_tensor(f"gate_{name}", shape, dt))

        featT = sb("featT", [P, TB * KB, P])
        logits, expd, w_sb = (sb(n, [P, TB, E]) for n in ("logits", "expd", "w_sb"))
        top, total, inv = (sb(n, [P, TB]) for n in ("top", "total", "inv"))
        wT_sb = sb("wT_sb", [E, TB * P])
        bn_cols = [sb(f"bn_cols{i}", [P, 5, EK]) for i in range(2)]
        bn_eps, bn_rsqrt, bn_diff = (sb(n, [P, 2, EK]) for n in ("bn_eps", "bn_rsqrt", "bn_diff"))
        wo_stage = sb("wo_stage", [P, E, KB * D])
        banks = [ctx.enter_context(nc.psum_tensor(f"gate_ps{i}", [P, 2, BANK], FP32)) for i in range(4)]

        wo_in = [ctx.enter_context(nc.semaphore(f"wo_in{i}")) for i in range(2)]
        names = """featT_psum featT_ready logits_psum logits_ready top_ready centred_ready exp_ready total_ready
            inv_ready w_ready wT_psum wT_ready table_psum table_ready spread_psum spread_ready
            bn_psum bn_cols_ready bn_eps_ready bn_rsqrt_ready bn_scale_ready bn_diff_ready bn_prod_ready
            wo_hi_ready""".split()
        S = {n: ctx.enter_context(nc.semaphore(f"gate_{n}")) for n in names}

        block = ctx.enter_context(nc.Block())

        @block.sync
        def _(sp):
            for i in range(2):
                h = slice(i * E // 2, (i + 1) * E // 2)
                sp.dma_start(wo_stage[:, h, :].rearrange("p e (k d) -> p e k d", k=KB),
                             Wo[h].rearrange("e (k p) d -> p e k d", p=P)).then_inc(wo_in[i], DMA)

        @block.tensor
        def _(pe):
            for it in range(TB):
                for d in range(KB):
                    i = it * KB + d
                    last = pe.transpose(banks[i // 8][:, (i % 8) // 4, (i % 4) * P:(i % 4 + 1) * P],
                                        node_table[:, it, d * P:(d + 1) * P], ident[:, :])
            last.then_inc(S["featT_psum"], 1)
            for i in range(2):
                last = pe.transpose(banks[3][:, i, 0:5 * EK], bn_rows[i][:, :], ident[0:5 * EK, 0:5 * EK])
            last.then_inc(S["bn_psum"], 1)
            pe.wait_ge(S["featT_ready"], 1)
            for it in range(TB):
                for d in range(KB):
                    last = pe.matmul(banks[2][:, 0, it * E:(it + 1) * E], featT[:, it * KB + d, :], wr_sb[:, d, :],
                                     start=(d == 0), stop=(d == KB - 1))
            last.then_inc(S["logits_psum"], 1)
            pe.wait_ge(S["w_ready"], 1)
            for it in range(TB):
                last = pe.transpose(banks[2][0:E, it // CT, (it % CT) * P:(it % CT + 1) * P], w_sb[:, it, :], ident[:, :])
            last.then_inc(S["wT_psum"], 1)
            pe.wait_ge(S["wT_ready"], 1)
            for it in range(TB):
                last = pe.matmul(banks[it // 4][:, (it % 4) // 2, (it % 2) * D:(it % 2 + 1) * D],
                                 wT_sb[:, it * P:(it + 1) * P], bo_sb[:, :], start=True, stop=True)
            last.then_inc(S["table_psum"], 1)
            for e in range(E):
                if e == 0:
                    pe.wait_ge(S["bn_cols_ready"], 1)
                elif e == 1:
                    pass
                elif e == 2:
                    pe.wait_ge(S["table_ready"], 1)
                else:
                    pe.wait_ge(S["spread_ready"], e - 3)
                pair = banks[(3, 2, 0, 1)[e % 4]]
                if e >= 4:
                    pe.wait_ge(S["spread_ready"], e - 3)
                for it in range(TB):
                    last = pe.transpose(pair[:, it // CT, (it % CT) * P:(it % CT + 1) * P],
                                        w_sb[:, it, e:e + 1].to_broadcast([P, P]), ident[:, :])
                last.then_inc(S["spread_psum"], 1)

        @block.scalar
        def _(act):
            act.wait_ge(S["featT_psum"], 1)
            for i in range(2):
                last = act.activation(featT[:, i * 8:(i + 1) * 8, :].rearrange("p i c -> p (i c)"),
                                      banks[i][:, :, :].rearrange("p k c -> p (k c)"), ACT.Copy, scale=1.0 / B)
            last.then_inc(S["featT_ready"], 1)
            act.wait_ge(S["centred_ready"], 1)
            act.activation(expd[:, :, :], logits[:, :, :], ACT.Exp).then_inc(S["exp_ready"], 1)
            act.wait_ge(S["wT_psum"], 1)
            act.activation(wT_sb[:, :], banks[2][0:E, :, :].rearrange("e k c -> e (k c)"), ACT.Copy) \
                .then_inc(S["wT_ready"], 1)
            for e in range(E):
                act.wait_ge(S["spread_psum"], e + 1)
                pair = banks[(3, 2, 0, 1)[e % 4]]
                act.activation(w_bc[:, :, e, :], pair[:, :, :], ACT.Copy).then_inc(S["spread_ready"], 1)

        @block.gpsimd
        def _(pool):
            pool.wait_ge(S["bn_eps_ready"], 1)
            pool.tensor_tensor(bn_rsqrt[:, :, :].rearrange("p i c -> p (i c)"),
                               bn_eps[:, :, :].rearrange("p i c -> p (i c)"),
                               minus_half[:, 0:1].to_broadcast([P, 2 * EK]), ALU.pow).then_inc(S["bn_rsqrt_ready"], 1)

        @block.vector
        def _(dve):
            dve.wait_ge(S["bn_psum"], 1)
            for i in range(2):
                last = dve.tensor_copy(bn_cols[i][:, :, :].rearrange("p i c -> p (i c)"), banks[3][:, i, 0:5 * EK])
            last.then_inc(S["bn_cols_ready"], 1)
            dve.wait_ge(S["bn_cols_ready"], 1)
            BIAS, GAMMA, BETA, MEAN, VAR = range(5)
            for i in range(2):
                last = dve.tensor_scalar(bn_eps[:, i, :], bn_cols[i][:, VAR, :], BN_EPS, None, ALU.add)
            last.then_inc(S["bn_eps_ready"], 1)
            dve.wait_ge(S["logits_psum"], 1)
            dve.tensor_tensor(expd[:, :, :], banks[2][:, 0, 0:TB * E].rearrange("p (t e) -> p t e", e=E),
                              br_sb[:, :].unsqueeze(1).to_broadcast([P, TB, E]), ALU.add).then_inc(S["logits_ready"], 1)
            dve.wait_ge(S["logits_ready"], 1)
            dve.tensor_reduce(top[:, :], expd[:, :, :], AX.X, ALU.max).then_inc(S["top_ready"], 1)
            dve.wait_ge(S["top_ready"], 1)
            dve.tensor_tensor(logits[:, :, :], expd[:, :, :], top[:, :].unsqueeze(2).to_broadcast([P, TB, E]),
                              ALU.subtract).then_inc(S["centred_ready"], 1)
            dve.wait_ge(S["exp_ready"], 1)
            dve.tensor_reduce(total[:, :], expd[:, :, :], AX.X, ALU.add).then_inc(S["total_ready"], 1)
            dve.wait_ge(S["total_ready"], 1)
            dve.reciprocal(inv[:, :], total[:, :]).then_inc(S["inv_ready"], 1)
            dve.wait_ge(S["inv_ready"], 1)
            dve.tensor_tensor(w_sb[:, :, :], expd[:, :, :], inv[:, :].unsqueeze(2).to_broadcast([P, TB, E]),
                              ALU.mult).then_inc(S["w_ready"], 1)
            dve.wait_ge(S["bn_rsqrt_ready"], 1)
            for i in range(2):
                dve.tensor_tensor(bn_scale[i][:, :], bn_rsqrt[:, i, :], bn_cols[i][:, GAMMA, :], ALU.mult) \
                    .then_inc(S["bn_scale_ready"], 1)
                dve.tensor_tensor(bn_diff[:, i, :], bn_cols[i][:, BIAS, :], bn_cols[i][:, MEAN, :], ALU.subtract) \
                    .then_inc(S["bn_diff_ready"], 1)
            for i in range(2):
                dve.wait_ge(S["bn_scale_ready"], i + 1)
                dve.wait_ge(S["bn_diff_ready"], i + 1)
                dve.tensor_tensor(bn_eps[:, i, :], bn_diff[:, i, :], bn_scale[i][:, :], ALU.mult) \
                    .then_inc(S["bn_prod_ready"], 1)
            for i in range(2):
                dve.wait_ge(S["bn_prod_ready"], i + 1)
                dve.tensor_tensor(bn_shift[i][:, :], bn_eps[:, i, :], bn_cols[i][:, BETA, :], ALU.add)
            for i in range(2):
                h = slice(i * E // 2, (i + 1) * E // 2)
                dve.wait_ge(wo_in[i], DMA)
                dve.tensor_copy(wo_hi[:, h, :], wo_stage[:, h, :]).then_inc(S["wo_hi_ready"], 1)
            dve.wait_ge(S["table_psum"], 1)
            for i in range(2):
                last = dve.tensor_copy(node_table[:, i * CT:(i + 1) * CT, :].rearrange("p t d -> p (t d)"),
                                       banks[i][:, :, :].rearrange("p k c -> p (k c)"))
            last.then_inc(S["table_ready"], 1)
            for i in range(2):
                h = slice(i * E // 2, (i + 1) * E // 2)
                dve.wait_ge(S["wo_hi_ready"], i + 1)
                dve.tensor_tensor(wo_lo[:, h, :], wo_stage[:, h, :], bits(wo_hi[:, h, :]), ALU.subtract)


def ffn_block(nc, B, x1_dram, out, ident, minus_half, ln_eps, w_bo, w12_hi, w12_lo, wo_hi, wo_lo, w_bc, bn_scale, bn_shift):
    D = w_bo.shape[2]
    KB, E, CT = D // P, w_bc.shape[2], BANK // P
    CH = w_bc.shape[1]
    US = CH * E
    LOOK = 3

    ctx = ExitStack()
    with ctx:
        def sb(name, shape, dt=FP32):
            return ctx.enter_context(nc.sbuf_tensor(name, shape, dt))

        def ps(name):
            return ctx.enter_context(nc.psum_tensor(name, [P, KB, BANK], FP32))

        def sem(name):
            return ctx.enter_context(nc.semaphore(name))

        x1_sb = [sb(f"ffn_x1{i}", [P, CT, D]) for i in range(2)]
        xn_sb = sb("ffn_xn", [P, CT, D])
        stats, mv = sb("ffn_stats", [P, CT, 6]), sb("ffn_mv", [P, CT, 2])
        vareps, rstd = sb("ffn_vareps", [P, CT]), sb("ffn_rstd", [P, CT])
        xT_hi, xT_lo = sb("xT_hi", [P, KB, BANK], FP32R), sb("xT_lo", [P, KB, BANK], FP32R)
        h1 = sb("h1", [P, KB, BANK])
        h1_hi = [sb(f"h1_hi{i}", [P, KB, BANK], FP32R) for i in range(2)]
        h1_lo = [sb(f"h1_lo{i}", [P, KB, BANK], FP32R) for i in range(2)]
        h2 = sb("h2", [P, KB, BANK])
        h2_hi = [sb(f"h2_hi{i}", [P, KB, BANK], FP32R) for i in range(2)]
        h2_lo = [sb(f"h2_lo{i}", [P, KB, BANK], FP32R) for i in range(2)]
        yT_sb = sb("yT_sb", [P, KB, BANK])

        z1_ps, z2_ps, y_ps, turn_ps = ps("z1_ps"), ps("z2_ps"), ps("y_ps"), ps("turn_ps")

        x1_in = [sem(f"ffn_x1_in{i}") for i in range(2)]
        stored = [sem(f"ffn_stored{i}") for i in range(2)]
        names = """stat mv_ready vareps_ready rstd_ready xn_ready residual_ready xT_psum xT_hi_ready xT_lo_ready
            z1_ready h1_ready h1_hi_ready h1_lo_ready z2_ready relu2_ready gated_ready h2_hi_ready h2_lo_ready
            step_done yT_ready out_psum out_ready""".split()
        S = {n: sem(f"ffn_{n}") for n in names}

        def step_at(b, u, off, last):
            t = u + off
            ok = t >= 0 and (t < US or not last)
            return ok, (t // E) % CH, t % E, b * US + (t + 1)

        def next_tile(b, u, last):
            t = u // E + 1
            return t >= 1 and (t < CH or not last), t % CH, b * CH + (t + 1)

        block = ctx.enter_context(nc.Block())

        @block.sync
        def _(sp):
            def load(b, c):
                sp.dma_start(x1_sb[c][:, :, :], x1_dram[c, b]).then_inc(x1_in[c], DMA)

            def store(b, c, last):
                wait(sp, S["out_ready"], b * CH + (c + 1))
                sp.dma_start(out[b].rearrange("(c s p) d -> c p s d", c=CH, p=P)[c], x1_sb[c][:, :, :]) \
                    .then_inc(stored[c], DMA)
                if not last:
                    sp.wait_ge(stored[c], DMA * (b + 1))
                    load(b + 1, c)

            for c in range(CH):
                load(0, c)
            if B > 1:
                with sp.Fori(0, B - 1) as b:
                    for c in range(CH):
                        store(b, c, False)
            for c in range(CH):
                store(B - 1, c, True)
            for c in range(CH):
                sp.wait_ge(stored[c], DMA * B)

        @block.gpsimd
        def _(pool):
            def tile(b, c):
                n = b * CH + (c + 1)
                pool.wait_ge(S["mv_ready"], n)
                pool.tensor_tensor(vareps[:, :], mv[:, :, 1], ln_eps[:, 0:CT], ALU.add).then_inc(S["vareps_ready"], 1)
                pool.wait_ge(S["vareps_ready"], n)
                pool.tensor_tensor(rstd[:, :], vareps[:, :], minus_half[:, 0:CT], ALU.pow).then_inc(S["rstd_ready"], 1)
                pool.wait_ge(S["xn_ready"], n)
                pool.tensor_tensor(x1_sb[c][:, :, :], x1_sb[c][:, :, :], w_bo[:, c * CT:(c + 1) * CT, :], ALU.add) \
                    .then_inc(S["residual_ready"], 1)

            if B > 1:
                with pool.Fori(0, B - 1) as b:
                    for c in range(CH):
                        tile(b, c)
            for c in range(CH):
                tile(B - 1, c)

        @block.tensor
        def _(pe):
            def transpose_x(n):
                pe.wait_ge(S["xn_ready"], n)
                wait(pe, S["out_ready"], n - 2)
                for d in range(KB):
                    for s in range(CT):
                        last = pe.transpose(turn_ps[:, d, s * P:(s + 1) * P], xn_sb[:, s, d * P:(d + 1) * P], ident[:, :])
                last.then_inc(S["xT_psum"], 1)

            def transpose_y(n):
                pe.wait_ge(S["yT_ready"], n)
                for s in range(CT):
                    for d in range(KB):
                        at = (s % 2) * D + d * P
                        last = pe.transpose(turn_ps[:, s // 2, at:at + P], yT_sb[:, d, s * P:(s + 1) * P], ident[:, :])
                last.then_inc(S["out_psum"], 1)

            def layer(acc, w_hi, w_lo, x_hi, x_lo, first, last):
                for m in range(KB):
                    for k in range(KB):
                        at = slice(k * D + m * P, k * D + (m + 1) * P)
                        done = split_matmul(pe, acc[:, m, :], w_hi[:, at], w_lo[:, at], x_hi[:, k, :], x_lo[:, k, :],
                                            first and k == 0, last and k == KB - 1)
                return done

            def slot(b, u, last):
                ok, c, e, n = step_at(b, u, 3, last)
                if ok:
                    if e == 0:
                        pe.wait_ge(S["xT_lo_ready"], b * CH + ((u + 3) // E + 1))
                    wait(pe, S["h1_ready"], n - 1)
                    layer(z1_ps, w12_hi[:, 0, e, :], w12_lo[:, 0, e, :], xT_hi, xT_lo, True, True) \
                        .then_inc(S["z1_ready"], 1)
                ok, _, n = next_tile(b, u, last)
                if ok and u % E == 4:
                    transpose_x(n)
                if u >= 0 and u % E == E - 1:
                    transpose_y(b * CH + (u // E + 1))
                ok, c, e, n = step_at(b, u, 2, last)
                if ok:
                    pe.wait_ge(S["h1_lo_ready"], n)
                    wait(pe, S["relu2_ready"], n - 1)
                    layer(z2_ps, w12_hi[:, 1, e, :], w12_lo[:, 1, e, :], h1_hi[n_par(u + 2)], h1_lo[n_par(u + 2)],
                          True, True).then_inc(S["z2_ready"], 1)
                ok, c, e, n = step_at(b, u, 1, last)
                if ok:
                    pe.wait_ge(S["h2_lo_ready"], n)
                    if e == 0:
                        wait(pe, S["yT_ready"], b * CH + (u + 1) // E)
                    layer(y_ps, wo_hi[:, e, :], wo_lo[:, e, :], h2_hi[n_par(u + 1)], h2_lo[n_par(u + 1)],
                          e == 0, e == E - 1).then_inc(S["step_done"], 1)

            transpose_x(1)
            for u in range(-LOOK, 0):
                slot(0, u, B == 1)
            if B > 1:
                with pe.Fori(0, B - 1) as b:
                    for u in range(US):
                        slot(b, u, False)
            for u in range(US):
                slot(B - 1, u, True)

        @block.scalar
        def _(act):
            def split_x(n):
                act.wait_ge(S["xT_psum"], n)
                act.activation(xT_hi[:, :, :], turn_ps[:, :, :], ACT.Copy).then_inc(S["xT_hi_ready"], 1)

            def bn_relu(dst, src, layer, e, m):
                col = slice(e * KB + m, e * KB + m + 1)
                return act.activation(dst[:, m, :], src[:, m, :], ACT.Relu, bias=bn_shift[layer][:, col],
                                      scale=bn_scale[layer][:, col])

            def slot(b, u, last):
                if u >= 0 and u % E == E - 1:
                    act.wait_ge(S["step_done"], b * US + (u + 1))
                    act.activation(yT_sb[:, :, :], y_ps[:, :, :], ACT.Copy).then_inc(S["yT_ready"], 1)
                ok, c, e, n = step_at(b, u, 3, last)
                if ok:
                    act.wait_ge(S["z1_ready"], n)
                    wait(act, S["h1_lo_ready"], n - 1)
                    for m in range(KB):
                        done = bn_relu(h1, z1_ps, 0, e, m)
                    done.then_inc(S["h1_ready"], 1)
                    act.wait_ge(S["h1_ready"], n)
                    wait(act, S["z2_ready"], n - 2)
                    act.activation(h1_hi[n_par(u + 3)][:, :, :], h1[:, :, :], ACT.Copy).then_inc(S["h1_hi_ready"], 1)
                ok, _, n = next_tile(b, u, last)
                if ok and u % E == 4:
                    act.wait_ge(S["z1_ready"], b * US + (u + 3 + 1))
                    split_x(n)
                ok, c, e, n = step_at(b, u, 2, last)
                if ok:
                    act.wait_ge(S["z2_ready"], n)
                    wait(act, S["h2_lo_ready"], n - 1)
                    for m in range(KB):
                        done = bn_relu(h2, z2_ps, 1, e, m)
                    done.then_inc(S["relu2_ready"], 1)

            split_x(1)
            for u in range(-LOOK, 0):
                slot(0, u, B == 1)
            if B > 1:
                with act.Fori(0, B - 1) as b:
                    for u in range(US):
                        slot(b, u, False)
            for u in range(US):
                slot(B - 1, u, True)

        @block.vector
        def _(dve):
            def statistics(c, n, turn):
                dve.wait_ge(x1_in[c], DMA * turn)
                for s in range(CT):
                    dve.bn_stats(stats[:, s, :], x1_sb[c][:, s, :]).then_inc(S["stat"], 1)

            def mean_var(n, waited):
                if not waited:
                    dve.wait_ge(S["stat"], CT * n)
                for s in range(CT):
                    last = dve.bn_aggr(mv[:, s, :], stats[:, s, :])
                last.then_inc(S["mv_ready"], 1)

            def normalise(c, n):
                dve.wait_ge(S["rstd_ready"], n)
                for s in range(CT):
                    last = dve.tensor_scalar(xn_sb[:, s, :], x1_sb[c][:, s, :], mv[:, s, 0:1], rstd[:, s:s + 1],
                                             ALU.subtract, ALU.mult)
                last.then_inc(S["xn_ready"], 1)

            def split_x(n):
                dve.wait_ge(S["xT_hi_ready"], n)
                dve.tensor_tensor(xT_lo[:, :, :], turn_ps[:, :, :], bits(xT_hi[:, :, :]), ALU.subtract) \
                    .then_inc(S["xT_lo_ready"], 1)

            def slot(b, u, last):
                tile_ok, tc, tn = next_tile(b, u, last)
                ok, c, e, n = step_at(b, u, 3, last)
                if ok:
                    i = n_par(u + 3)
                    if tile_ok and u % E == 3:
                        dve.wait_ge(S["stat"], CT * tn)
                    dve.wait_ge(S["h1_hi_ready"], n)
                    dve.tensor_tensor(h1_lo[i][:, :, :], h1[:, :, :], bits(h1_hi[i][:, :, :]), ALU.subtract) \
                        .then_inc(S["h1_lo_ready"], 1)
                if tile_ok and u % E == 3:
                    mean_var(tn, ok)
                if tile_ok and u % E == 4:
                    split_x(tn)
                ok, c, e, n = step_at(b, u, 2, last)
                if ok:
                    i = n_par(u + 2)
                    dve.wait_ge(S["relu2_ready"], n)
                    dve.tensor_tensor(h2[:, :, :], h2[:, :, :], w_bc[:, c, e, :].unsqueeze(1).to_broadcast([P, KB, BANK]),
                                      ALU.mult).then_inc(S["gated_ready"], 1)
                    dve.wait_ge(S["gated_ready"], n)
                    wait(dve, S["step_done"], n - 2)
                    dve.tensor_copy(h2_hi[i][:, :, :], h2[:, :, :]).then_inc(S["h2_hi_ready"], 1)
                    dve.wait_ge(S["h2_hi_ready"], n)
                    dve.tensor_tensor(h2_lo[i][:, :, :], h2[:, :, :], bits(h2_hi[i][:, :, :]), ALU.subtract) \
                        .then_inc(S["h2_lo_ready"], 1)
                if u >= 0 and u % E == E - 1:
                    t = u // E
                    dve.wait_ge(S["out_psum"], b * CH + (t + 1))
                    dve.wait_ge(S["residual_ready"], b * CH + (t + 1))
                    rows = x1_sb[t][:, :, :].rearrange("p s d -> p (s d)")
                    dve.tensor_tensor(rows, turn_ps[:, :, :].rearrange("p k c -> p (k c)"), rows, ALU.add) \
                        .then_inc(S["out_ready"], 1)
                if tile_ok and u % E == 2:
                    statistics(tc, tn, b + (u // E + 1) // CH + 1)
                if tile_ok and u % E == 3:
                    normalise(tc, tn)

            statistics(0, 1, 1)
            mean_var(1, False)
            normalise(0, 1)
            split_x(1)
            for u in range(-LOOK, 0):
                slot(0, u, B == 1)
            if B > 1:
                with dve.Fori(0, B - 1) as b:
                    for u in range(US):
                        slot(b, u, False)
            for u in range(US):
                slot(B - 1, u, True)


def n_par(t):
    return t % 2


INPUTS = ["x", "adj", "L0_gnn_W", "L0_gnn_a", "L0_ffn_Wr", "L0_ffn_br",
          "L0_ffn_W1", "L0_ffn_b1", "L0_ffn_g1", "L0_ffn_be1", "L0_ffn_m1", "L0_ffn_v1",
          "L0_ffn_W2", "L0_ffn_b2", "L0_ffn_g2", "L0_ffn_be2", "L0_ffn_m2", "L0_ffn_v2", "L0_ffn_Wo", "L0_ffn_bo"]


def kernel(**inputs):
    import numpy as np
    import concourse.bacc as bacc
    from concourse.bass_utils import run_bass_kernel_spmd

    nc = bacc.Bacc("TRN2", target_bir_lowering=False, num_devices=1)
    arrays, args = {}, []
    for name in INPUTS:
        array = np.ascontiguousarray(inputs[name])
        arrays[f"in_{name}"] = array
        args.append(nc.dram_tensor(f"in_{name}", array.shape, mybir.dt.from_np(array.dtype), kind="ExternalInput").ap())
    args.append(nc.dram_tensor("out", arrays["in_x"].shape, FP32, kind="ExternalOutput").ap())
    program(nc, *args)
    result = run_bass_kernel_spmd(nc, [arrays], core_ids=[0])
    return result.results[0]["out"]
```

```python
from contextlib import ExitStack

import concourse.bass as bass
import concourse.mybir as mybir

FP32 = mybir.dt.float32
FP32R = mybir.dt.float32r
BF16 = mybir.dt.bfloat16
INT32 = mybir.dt.int32
ALU = mybir.AluOpType
ACT = mybir.ActivationFunctionType
AX = mybir.AxisListType

P = 128
BANK = 512
LN_EPS = 1e-5
BN_EPS = 1e-3
SLOPE = 0.2
EDGE_UNIT = 2.0 ** -64
TINY = 1e-30
DMA = 16


def wait(eng, sem, value):
    if isinstance(value, int) and value <= 0:
        return
    eng.wait_ge(sem, value)


def bits(ap):
    return ap.bitcast(FP32)


def split_matmul(pe, out, w_hi, w_lo, x_hi, x_lo, first, last):
    pe.matmul(out, w_hi, x_hi, start=first, stop=False)
    pe.matmul(out, w_hi, x_lo, start=False, stop=False)
    return pe.matmul(out, w_lo, x_hi, start=False, stop=last)


def program(nc, x, adj, W, a, Wr, br, W1, b1, g1, be1, m1, v1, W2, b2, g2, be2, m2, v2, Wo, bo, out):
    B, N, D = x.shape
    E = Wr.shape[1]
    KB = D // P
    TB = N // P
    PAIRS = B // 2
    UT = 2 * TB
    CT = BANK // P
    CH = N // BANK
    US = CH * E
    DX = D + 2
    assert B % 2 == 0 and D == 2 * P and CH == 2 and E == 8 and TB == 8

    x1_dram = nc.dram_tensor("x1_scratch", [CH, B, P, CT, D], FP32, kind="Internal").ap()

    persistent = ExitStack()
    with persistent:
        def keep(name, shape, dt=FP32):
            return persistent.enter_context(nc.sbuf_tensor(name, shape, dt))

        ident = keep("ident", [P, P])
        minus_half, ln_eps = keep("minus_half", [P, CT]), keep("ln_eps", [P, CT])
        w12_hi = keep("w12_hi", [P, 2, E, KB * D], FP32R)
        w12_lo = keep("w12_lo", [P, 2, E, KB * D], FP32R)
        node_table = keep("node_table", [P, TB, D])
        wr_sb = keep("wr_sb", [P, KB, E])
        br_sb = keep("br_sb", [P, E])
        bo_sb = keep("bo_sb", [E, D])
        bn_rows = [keep(f"bn_rows{i}", [5 * E * KB, P]) for i in range(2)]

        attention_block(nc, x, adj, W, a, W1, W2, x1_dram, ident, minus_half, ln_eps, w12_hi, w12_lo, node_table,
                        (Wr, br, bo, (b1, g1, be1, m1, v1), (b2, g2, be2, m2, v2)),
                        (wr_sb, br_sb, bo_sb, bn_rows))

        w_bc = keep("w_bc", [P, CH, E, BANK])
        wo_hi = keep("wo_hi", [P, E, KB * D], FP32R)
        wo_lo = keep("wo_lo", [P, E, KB * D], FP32R)
        bn_scale = [keep(f"bn_scale{i}", [P, E * KB]) for i in range(2)]
        bn_shift = [keep(f"bn_shift{i}", [P, E * KB]) for i in range(2)]
        gate_block(nc, B, Wo, ident, minus_half, node_table, wr_sb, br_sb, bo_sb, bn_rows,
                   w_bc, wo_hi, wo_lo, bn_scale, bn_shift)
        ffn_block(nc, B, x1_dram, out, ident, minus_half, ln_eps, node_table, w12_hi, w12_lo, wo_hi, wo_lo,
                  w_bc, bn_scale, bn_shift)


def attention_block(nc, x, adj, W, a, W1, W2, x1_dram, ident, minus_half, ln_eps, w12_hi, w12_lo, feat_sum,
                    small_dram, small_sb):
    B, N, D = x.shape
    E = W1.shape[0]
    KB, TB, PAIRS = D // P, N // P, B // 2
    UT, CT = 2 * TB, BANK // P
    DX = D + 2
    HEADS = TB // 2
    Wr, br, bo, bn1, bn2 = small_dram
    wr_sb, br_sb, bo_sb, bn_rows = small_sb
    assert 2 * E == UT

    ctx = ExitStack()
    with ctx:
        def sb(name, shape, dt=FP32):
            return ctx.enter_context(nc.sbuf_tensor(name, shape, dt))

        def ps(name, shape, dt=FP32):
            return ctx.enter_context(nc.psum_tensor(name, shape, dt))

        def sem(name):
            return ctx.enter_context(nc.semaphore(name))

        w_sb = sb("w_sb", [P, KB, D])
        a_sb = sb("a_sb", [P, KB, 2])
        wx = sb("wx", [P, KB, DX])
        x_sb = [sb(f"x_sb{i}", [P, TB, D]) for i in range(2)]
        adj_sb = [sb(f"adj_sb{i}", [P, N], INT32) for i in range(2)]
        ej_rows = [sb(f"ej_rows{i}", [P, N]) for i in range(2)]
        scores = [sb(f"scores{i}", [P, N]) for i in range(4)]
        upper = [sb(f"upper{i}", [P, N]) for i in range(2)]
        pT_hi = [sb(f"pT_hi{i}", [P, TB, P], FP32R) for i in range(2)]
        pT_lo = [sb(f"pT_lo{i}", [P, TB, P], FP32R) for i in range(2)]
        wh_hi = [sb(f"wh_hi{i}", [P, TB, D], FP32R) for i in range(2)]
        wh_lo = [sb(f"wh_lo{i}", [P, TB, D], FP32R) for i in range(2)]
        e_cols = [sb(f"e_cols{i}", [P, TB, 2]) for i in range(2)]
        row_max, neg_max = (sb(n, [P, 4]) for n in ("row_max", "neg_max"))
        row_sum, row_den, row_inv = (sb(n, [P, 4]) for n in ("row_sum", "row_den", "row_inv"))
        x1_sb = [sb(f"x1_sb{i}", [P, D]) for i in range(4)]
        x1_stats, x1_mv = sb("x1_stats", [P, 2, 6]), sb("x1_mv", [P, 4, 2])
        x1_vareps, x1_rstd = sb("x1_vareps", [P, 4]), sb("x1_rstd", [P, 4])
        n1_sb = [sb(f"n1_sb{i}", [P, D]) for i in range(2)]
        xs_stats, xs_mv = sb("xs_stats", [P, 2, 6]), sb("xs_mv", [P, 2, 2, 2])
        xs_vareps, xs_rstd = sb("xs_vareps", [P, 2, 2]), sb("xs_rstd", [P, 2, 2])
        w_stats, w_mv, w_centred = sb("w_stats", [P, KB, 6]), sb("w_mv", [P, KB, 2]), sb("w_centred", [P, KB, D])
        hT = sb("hT", [P, KB, 2 * P])
        w_stage = [sb(f"w_stage{i}", [P, KB * D]) for i in range(2)]

        pT_ps = [ps(f"pT_ps{i}", [P, TB, P]) for i in range(2)]
        attn_ps = [ps(f"attn_ps{i}", [P, BANK]) for i in range(2)]
        head_ps = ps("head_ps", [P, 2, BANK])

        small_in = sem("small_in")
        w_in = sem("w_in")
        x_in = [[sem(f"x_in{i}{h}") for h in range(2)] for i in range(2)]
        adj_in = [sem(f"adj_in{i}") for i in range(2)]
        stage_in = [[sem(f"w{layer + 1}_stage_in{i}") for i in range(2)] for layer in range(2)]
        x1_stored = [sem(f"x1_stored{i}") for i in range(4)]
        names = """const_zero const_ready w_stat w_mv_ready w_centred_ready a_scaled wT_ready wx_ready
            xs_stat xs_mv_ready xs_vareps_ready xs_rstd_ready hT_psum hT_ready
            wh_ready wh_hi_ready wh_lo_ready ej_rows_psum ej_rows_ready
            masked_ready upper_ready lrelu_ready negmax_ready probs_ready
            pT_ready pT_hi_ready pT_lo_ready attn_ready den_ready inv_ready x1_ready
            x1_stat x1_mv_ready x1_vareps_ready x1_rstd_ready n1_ready n1_added
            w12_hi_ready w12_lo_ready""".split()
        S = {n: sem(n) for n in names}

        def tile_at(k, u, off, last):
            t = u + off
            ok = (t >= 0 or not isinstance(k, int)) and (t < UT or not last)
            return ok, t, k * UT + (t + 1)

        def head_at(k, u, last):
            g = u + 3
            if g < 0:
                return None
            off = g // TB + 1
            return None if last and off >= 2 else (off, g % TB)

        def parity(t):
            return (t // TB) % 2

        block = ctx.enter_context(nc.Block())

        @block.sync
        def _(sp):
            sp.dma_start(w_sb[:, :, :], W.rearrange("(o p) d -> p o d", p=P)).then_inc(w_in, DMA)
            for h in range(2):
                sp.dma_start(a_sb[:, :, h], a.rearrange("(h o p) -> h p o", p=P, o=KB)[h],
                             allow_slow_non_contiguous=True).then_inc(w_in, DMA)

            def load_x(b, i, half):
                h = slice(half * TB // 2, (half + 1) * TB // 2)
                sp.dma_start(x_sb[i][:, h, :], x[b].rearrange("(t p) d -> p t d", p=P)[:, h, :]) \
                    .then_inc(x_in[i][half], DMA)

            def load_adj(b, it, i):
                sp.dma_start(adj_sb[i][:, :], adj[b, it * P:(it + 1) * P, :]).then_inc(adj_in[i], DMA)

            for half in range(2):
                load_x(0, 0, half)
            load_adj(0, 0, 0)
            load_adj(0, 1, 1)
            for half in range(2):
                load_x(1, 1, half)
            sp.dma_start(wr_sb[:, :, :], Wr.rearrange("(k p) e -> p k e", p=P),
                         allow_slow_non_contiguous=True).then_inc(small_in, DMA)
            sp.dma_start(br_sb[:, :], br.partition_broadcast(P)).then_inc(small_in, DMA)
            sp.dma_start(bo_sb[:, :], bo[:, :]).then_inc(small_in, DMA)
            for rows, params in zip(bn_rows, (bn1, bn2)):
                for i, p in enumerate(params):
                    sp.dma_start(rows[i * E * KB:(i + 1) * E * KB, :],
                                 p.rearrange("e (k p) -> (e k) p", p=P)).then_inc(small_in, DMA)

            def slot(k, u, last):
                ok, t, n = tile_at(k, u, 7, last)
                if ok:
                    wait(sp, S["masked_ready"], n - 2)
                    load_adj(2 * k + t // TB, t % TB, t % 2)
                ok, t, n = tile_at(k, u, 0, last)
                if ok and t >= 0:
                    wait(sp, S["x1_ready"], n)
                    it = t % TB
                    sp.dma_start(x1_dram[it // CT, 2 * k + t // TB, :, it % CT, :],
                                 x1_sb[t % 4][:, :]).then_inc(x1_stored[t % 4], DMA)
                    if not last and it % CT == CT - 1:
                        load_x(2 * k + t // TB + 2, t // TB, it // CT)

            for u in range(-5, 0):
                slot(0, u, PAIRS == 1)
            if PAIRS > 1:
                with sp.Fori(0, PAIRS - 1) as k:
                    for u in range(UT):
                        slot(k, u, False)
            for u in range(UT):
                slot(PAIRS - 1, u, True)
            for i in range(4):
                sp.wait_ge(x1_stored[i], DMA * (1 + PAIRS * UT // 4))
            sp.wait_ge(small_in, DMA * 13)

        @block.gpsimd
        def _(pool):
            for i in range(4):
                pool.sem_inc(x1_stored[i], DMA)
            pool.sem_inc(S["n1_ready"], 4)
            pool.sem_inc(S["n1_added"], 1)
            pool.memset(ident[:, :], 0.0).then_inc(S["const_zero"], 1)
            pool.memset(minus_half[:, :], -0.5)
            pool.memset(ln_eps[:, :], LN_EPS)
            pool.memset(feat_sum[:, :, :], 0.0)
            pool.wait_ge(S["const_zero"], 1)
            pool.affine_select(out=ident[:, :], in_=ident[:, :], compare_op=ALU.not_equal, fill=1.0, base=0,
                               pattern=[[-1, P]], channel_multiplier=1).then_inc(S["const_ready"], 1)

            def head_rstd(c, step):
                i = step % 2
                pool.wait_ge(S["xs_mv_ready"], c)
                pool.tensor_tensor(xs_vareps[:, i, :], xs_mv[:, i, :, 1], ln_eps[:, 0:2], ALU.add) \
                    .then_inc(S["xs_vareps_ready"], 1)
                pool.wait_ge(S["xs_vareps_ready"], c)
                pool.tensor_tensor(xs_rstd[:, i, :], xs_vareps[:, i, :], minus_half[:, 0:2], ALU.pow) \
                    .then_inc(S["xs_rstd_ready"], 1)

            def load_weights(task):
                pool.dma_start(w_stage[task % 2][:, :].rearrange("p (k d) -> p k d", k=KB),
                               W1[task].rearrange("(k p) d -> p k d", p=P)).then_inc(stage_in[0][task % 2], DMA)

            def split_weights(task):
                layer, e, stage = task // E, task % E, w_stage[task % 2]
                pool.wait_ge(stage_in[layer][task % 2], DMA * (e // 2 + 1))
                pool.tensor_copy(w12_hi[:, layer, e, :], stage[:, :]).then_inc(S["w12_hi_ready"], 1)
                pool.wait_ge(S["w12_hi_ready"], task + 1)
                pool.tensor_tensor(w12_lo[:, layer, e, :], stage[:, :], bits(w12_hi[:, layer, e, :]),
                                   ALU.subtract).then_inc(S["w12_lo_ready"], 1)

            def slot(k, u, last):
                head = head_at(k, u, last)
                if head and 1 <= head[1] <= HEADS:
                    head_rstd((2 * k + head[0]) * HEADS + head[1], head[1] - 1)
                ok, t, n = tile_at(k, u, 1, last)
                if ok:
                    pool.wait_ge(S["x1_mv_ready"], n)
                    pool.tensor_tensor(x1_vareps[:, t % 4:t % 4 + 1], x1_mv[:, t % 4, 1:2], ln_eps[:, 0:1], ALU.add) \
                        .then_inc(S["x1_vareps_ready"], 1)
                    pool.wait_ge(S["x1_vareps_ready"], n)
                    pool.tensor_tensor(x1_rstd[:, t % 4:t % 4 + 1], x1_vareps[:, t % 4:t % 4 + 1],
                                       minus_half[:, 0:1], ALU.pow).then_inc(S["x1_rstd_ready"], 1)
                ok0, t0, n0 = tile_at(k, u, 0, last)
                ok0 = ok0 and t0 >= 0
                ok1, t1, n1 = tile_at(k, u, 1, last)
                if ok0:
                    pool.wait_ge(S["n1_ready"], n0 + 4)
                    if ok1:
                        pool.wait_ge(S["x1_rstd_ready"], n1)
                    pool.wait_ge(S["n1_added"], n0)
                    rows = feat_sum[:, t0 % TB, :]
                    pool.tensor_tensor(rows, rows, n1_sb[t0 % 2][:, :], ALU.add).then_inc(S["n1_added"], 1)
                if ok1:
                    if not ok0:
                        pool.wait_ge(S["x1_rstd_ready"], n1)
                    pool.tensor_scalar(n1_sb[t1 % 2][:, :], x1_sb[t1 % 4][:, :], x1_mv[:, t1 % 4, 0:1],
                                       x1_rstd[:, t1 % 4:t1 % 4 + 1], ALU.subtract, ALU.mult) \
                        .then_inc(S["n1_ready"], 1)
                if last and u >= 0 and u % 2 == 0:
                    split_weights(E + u // 2)

            load_weights(0)
            for task in range(E):
                if task > 0:
                    pool.wait_ge(S["w12_lo_ready"], task)
                if task + 1 < E:
                    load_weights(task + 1)
                split_weights(task)
                if task % 2 == 0:
                    head_rstd(task // 2 + 1, task // 2)
            for u in range(-5, 0):
                slot(0, u, PAIRS == 1)
            if PAIRS > 1:
                with pool.Fori(0, PAIRS - 1) as k:
                    for u in range(UT):
                        slot(k, u, False)
            for u in range(UT):
                slot(PAIRS - 1, u, True)

        @block.tensor
        def _(pe):
            pe.wait_ge(S["const_ready"], 1)
            pe.wait_ge(S["w_centred_ready"], 1)
            pe.wait_ge(S["a_scaled"], 1)
            for d in range(KB):
                for o in range(KB):
                    pe.transpose(head_ps[:, d, o * P:(o + 1) * P], w_centred[:, o, d * P:(d + 1) * P], ident[:, :])
                for o in range(KB):
                    last = pe.matmul(head_ps[:, d, D:DX], w_centred[:, o, d * P:(d + 1) * P], a_sb[:, o, :],
                                     start=(o == 0), stop=(o == KB - 1))
            last.then_inc(S["wT_ready"], 1)
            pe.wait_ge(S["wx_ready"], 1)

            def head_transpose(b, j, i, turn):
                if j == 0:
                    wait(pe, S["ej_rows_ready"], b)
                else:
                    pe.wait_ge(S["wh_lo_ready"], b * TB + 2 * j)
                if j % 2 == 0:
                    pe.wait_ge(x_in[i][j // 2], DMA * turn)
                for c in range(2):
                    for d in range(KB):
                        at = d * 2 * P + c * P
                        last = pe.transpose(head_ps[:, 0, at:at + P], x_sb[i][:, 2 * j + c, d * P:(d + 1) * P],
                                            ident[:, :])
                last.then_inc(S["hT_psum"], 1)

            def head_project(b, j):
                pe.wait_ge(S["hT_ready"], b * HEADS + (j + 1))
                for c in range(2):
                    for d in range(KB):
                        cols = slice(c * P, (c + 1) * P)
                        last = pe.matmul(head_ps[:, 1 - c, 0:DX], hT[:, d, cols], wx[:, d, :],
                                         start=(d == 0), stop=(d == KB - 1))
                    last.then_inc(S["wh_ready"], 1)

            def spread_ej(b, i):
                pe.wait_ge(S["wh_lo_ready"], b * TB + TB)
                for t in range(TB):
                    at = (t % CT) * P
                    last = pe.transpose(head_ps[:, t // CT, at:at + P],
                                        e_cols[i][:, t, 1:2].to_broadcast([P, P]), ident[:, :])
                last.then_inc(S["ej_rows_psum"], 1)

            def slot(k, u, last_pair):
                head = head_at(k, u, last_pair)
                if head and head[1] == HEADS + 1:
                    spread_ej(2 * k + head[0], head[0] % 2)
                ok, t, n = tile_at(k, u, 3, last_pair)
                if ok:
                    pe.wait_ge(S["probs_ready"], n)
                    wait(pe, S["pT_lo_ready"], n - 2)
                    for j in range(TB):
                        last = pe.transpose(pT_ps[t % 2][:, j, :], scores[t % 4][:, j * P:(j + 1) * P], ident[:, :])
                    last.then_inc(S["pT_ready"], 1)
                if head and 1 <= head[1] <= HEADS:
                    head_project(2 * k + head[0], head[1] - 1)
                ok, t, n = tile_at(k, u, 2, last_pair)
                if ok:
                    pe.wait_ge(S["pT_lo_ready"], n)
                    wait(pe, S["x1_ready"], n - 2)
                    i, acc = parity(t), attn_ps[t % 2][:, 0:D]
                    for j in range(TB):
                        last = split_matmul(pe, acc, pT_hi[t % 2][:, j, :], pT_lo[t % 2][:, j, :],
                                            wh_hi[i][:, j, :], wh_lo[i][:, j, :], j == 0, j == TB - 1)
                    last.then_inc(S["attn_ready"], 1)
                if head and head[1] < HEADS:
                    head_transpose(2 * k + head[0], head[1], head[0] % 2, k + (head[0] // 2 + 1))

            for j in range(HEADS):
                head_transpose(0, j, 0, 1)
                head_project(0, j)
            spread_ej(0, 0)
            for u in range(-5, 0):
                slot(0, u, PAIRS == 1)
            if PAIRS > 1:
                with pe.Fori(0, PAIRS - 1) as k:
                    for u in range(UT):
                        slot(k, u, False)
            for u in range(UT):
                slot(PAIRS - 1, u, True)

        @block.scalar
        def _(act):
            act.wait_ge(S["wT_ready"], 1)
            act.activation(wx[:, :, :], head_ps[:, :, 0:DX], ACT.Copy).then_inc(S["wx_ready"], 1)

            def head_hT(b, j):
                act.wait_ge(S["hT_psum"], b * HEADS + (j + 1))
                act.activation(hT[:, :, :].rearrange("p k c -> p (k c)"), head_ps[:, 0, :], ACT.Copy) \
                    .then_inc(S["hT_ready"], 1)

            def head_wh(b, j, i):
                act.wait_ge(S["xs_rstd_ready"], b * HEADS + (j + 1))
                for c in range(2):
                    t = 2 * j + c
                    act.wait_ge(S["wh_ready"], b * TB + (t + 1))
                    act.activation(e_cols[i][:, t, :], head_ps[:, 1 - c, D:DX], ACT.Copy,
                                   scale=xs_rstd[:, j % 2, c:c + 1])
                    act.activation(wh_hi[i][:, t, :], head_ps[:, 1 - c, 0:D], ACT.Copy,
                                   scale=xs_rstd[:, j % 2, c:c + 1]).then_inc(S["wh_hi_ready"], 1)

            def head_ej(b, i):
                act.wait_ge(S["ej_rows_psum"], b + 1)
                act.activation(ej_rows[i][:, :], head_ps[:, :, :].rearrange("p k c -> p (k c)"), ACT.Copy,
                               scale=-EDGE_UNIT).then_inc(S["ej_rows_ready"], 1)

            def load_w2(task):
                act.wait_ge(S["w12_lo_ready"], task - 1)
                act.dma_start(w_stage[task % 2][:, :].rearrange("p (k d) -> p k d", k=KB),
                              W2[task - E].rearrange("(k p) d -> p k d", p=P)).then_inc(stage_in[1][task % 2], DMA)

            def slot(k, u, last):
                head = head_at(k, u, last)
                if head and 1 <= head[1] <= HEADS:
                    head_hT(2 * k + head[0], head[1] - 1)
                if head and head[1] == HEADS + 1:
                    head_ej(2 * k + head[0], head[0] % 2)
                ok, t, n = tile_at(k, u, 5, last)
                if ok:
                    act.wait_ge(S["masked_ready"], n)
                    wait(act, S["lrelu_ready"], n - 2)
                    act.activation(upper[t % 2][:, :], scores[t % 4][:, :], ACT.Relu, scale=1.0 - 1.0 / SLOPE,
                                   bias=e_cols[parity(t)][:, t % TB, 0:1]).then_inc(S["upper_ready"], 1)
                ok, t, n = tile_at(k, u, 3, last)
                if ok:
                    act.wait_ge(S["pT_ready"], n)
                    wait(act, S["attn_ready"], n - 2)
                    act.activation(pT_hi[t % 2][:, :, :], pT_ps[t % 2][:, :, :], ACT.Copy) \
                        .then_inc(S["pT_hi_ready"], 1)
                ok, t, n = tile_at(k, u, 4, last)
                if ok:
                    s, c = scores[t % 4], t % 4
                    act.wait_ge(S["negmax_ready"], n)
                    act.activation(s[:, :], s[:, :], ACT.Exp, bias=neg_max[:, c:c + 1],
                                   accum_out=row_sum[:, c:c + 1]).then_inc(S["probs_ready"], 1)
                if head and 1 <= head[1] <= HEADS:
                    head_wh(2 * k + head[0], head[1] - 1, head[0] % 2)
                if last and u >= 0 and u % 2 == 0 and E + u // 2 + 1 < 2 * E:
                    load_w2(E + u // 2 + 1)

            for j in range(HEADS):
                head_hT(0, j)
                head_wh(0, j, 0)
            head_ej(0, 0)
            for u in range(-5, 0):
                slot(0, u, PAIRS == 1)
            if PAIRS > 1:
                with act.Fori(0, PAIRS - 1) as k:
                    for u in range(UT):
                        slot(k, u, False)
            load_w2(E)
            for u in range(UT):
                slot(PAIRS - 1, u, True)

        @block.vector
        def _(dve):
            dve.wait_ge(w_in, 3 * DMA)
            for o in range(KB):
                dve.bn_stats(w_stats[:, o, :], w_sb[:, o, :]).then_inc(S["w_stat"], 1)
            dve.wait_ge(S["w_stat"], KB)
            for o in range(KB):
                dve.bn_aggr(w_mv[:, o, :], w_stats[:, o, :]).then_inc(S["w_mv_ready"], 1)
            dve.wait_ge(S["w_mv_ready"], KB)
            for o in range(KB):
                last = dve.tensor_scalar(w_centred[:, o, :], w_sb[:, o, :], w_mv[:, o, 0:1], None, ALU.subtract)
            last.then_inc(S["w_centred_ready"], 1)
            dve.tensor_scalar(a_sb[:, :, 0], a_sb[:, :, 0], (1.0 / SLOPE - 1.0) * EDGE_UNIT, None, ALU.mult) \
                .then_inc(S["a_scaled"], 1)

            def head_stats(b, j, i, turn):
                if j % 2 == 0:
                    dve.wait_ge(x_in[i][j // 2], DMA * turn)
                for c in range(2):
                    dve.bn_stats(xs_stats[:, c, :], x_sb[i][:, 2 * j + c, :]).then_inc(S["xs_stat"], 1)

            def head_mean_var(b, j, waited):
                if not waited:
                    dve.wait_ge(S["xs_stat"], 2 * (b * HEADS + (j + 1)))
                for c in range(2):
                    last = dve.bn_aggr(xs_mv[:, j % 2, c, :], xs_stats[:, c, :])
                last.then_inc(S["xs_mv_ready"], 1)

            def head_wh(b, j, i):
                for c in range(2):
                    t, rstd = 2 * j + c, xs_rstd[:, j % 2, c:c + 1]
                    dve.wait_ge(S["wh_hi_ready"], b * TB + (t + 1))
                    dve.scalar_tensor_tensor(wh_lo[i][:, t, :], head_ps[:, 1 - c, 0:D], rstd, bits(wh_hi[i][:, t, :]),
                                             ALU.mult, ALU.subtract).then_inc(S["wh_lo_ready"], 1)

            def slot(k, u, last):
                head = head_at(k, u, last)
                step = head[1] if head else None
                hb, hi = (2 * k + head[0], head[0] % 2) if head else (None, None)
                post, pt, pn = tile_at(k, u, 1, last)
                pc = pt % 4
                ok, t, n = tile_at(k, u, 5, last)
                if ok:
                    dve.wait_ge(adj_in[t % 2], DMA * (k * (UT // 2) + (t // 2 + 1)))
                    if t % TB == 0:
                        dve.wait_ge(S["ej_rows_ready"], 2 * k + (t // TB + 1))
                    wait(dve, S["pT_ready"], n - 4)
                    dve.scalar_tensor_tensor(scores[t % 4][:, :], adj_sb[t % 2][:, :], 0.0, ej_rows[parity(t)][:, :],
                                             ALU.is_equal, ALU.add).then_inc(S["masked_ready"], 1)
                stats = bool(head) and 1 <= step <= HEADS
                if stats:
                    head_stats(hb, step - 1, hi, k + (head[0] // 2 + 1))
                ok, t, n = tile_at(k, u, 4, last)
                if ok:
                    c = t % 4
                    if post:
                        dve.wait_ge(S["probs_ready"], pn)
                        dve.wait_ge(S["upper_ready"], n)
                        if stats:
                            dve.wait_ge(S["xs_stat"], 2 * (hb * HEADS + step))
                        sum_to_den(pc)
                    else:
                        dve.wait_ge(S["upper_ready"], n)
                    if stats:
                        head_mean_var(hb, step - 1, post)
                    dve.tensor_tensor_reduce(out=scores[c][:, :], in0=upper[t % 2][:, :], in1=scores[c][:, :],
                                             scale=SLOPE / EDGE_UNIT, scalar=-0.5 * SLOPE / EDGE_UNIT,
                                             op0=ALU.subtract, op1=ALU.max, accum_out=row_max[:, c:c + 1]) \
                        .then_inc(S["lrelu_ready"], 1)
                else:
                    assert not stats
                    if post:
                        dve.wait_ge(S["probs_ready"], pn)
                        sum_to_den(pc)
                if post:
                    dve.wait_ge(S["den_ready"], pn)
                    dve.reciprocal(row_inv[:, pc:pc + 1], row_den[:, pc:pc + 1]).then_inc(S["inv_ready"], 1)
                if ok:
                    dve.wait_ge(S["lrelu_ready"], n)
                    dve.tensor_scalar(neg_max[:, c:c + 1], row_max[:, c:c + 1], -1.0, None, ALU.mult) \
                        .then_inc(S["negmax_ready"], 1)
                if post:
                    dve.wait_ge(S["inv_ready"], pn)
                    dve.wait_ge(S["attn_ready"], pn)
                    dve.wait_ge(x1_stored[pc], DMA * (k * (UT // 4) + (pt // 4 + 1)))
                    dve.wait_ge(S["n1_ready"], pn)
                    dve.scalar_tensor_tensor(x1_sb[pc][:, :], attn_ps[pt % 2][:, 0:D], row_inv[:, pc:pc + 1],
                                             x_sb[parity(pt)][:, pt % TB, :], ALU.mult, ALU.add) \
                        .then_inc(S["x1_ready"], 1)
                    dve.wait_ge(S["x1_ready"], pn)
                    dve.bn_stats(x1_stats[:, pt % 2, :], x1_sb[pc][:, :]).then_inc(S["x1_stat"], 1)
                ok, t, n = tile_at(k, u, 3, last)
                if ok:
                    if post:
                        dve.wait_ge(S["x1_stat"], pn)
                    dve.wait_ge(S["pT_hi_ready"], n)
                    wait(dve, S["attn_ready"], n - 2)
                    dve.tensor_tensor(pT_lo[t % 2][:, :, :], pT_ps[t % 2][:, :, :], bits(pT_hi[t % 2][:, :, :]),
                                      ALU.subtract).then_inc(S["pT_lo_ready"], 1)
                if post:
                    if not ok:
                        dve.wait_ge(S["x1_stat"], pn)
                    dve.bn_aggr(x1_mv[:, pc, :], x1_stats[:, pt % 2, :]).then_inc(S["x1_mv_ready"], 1)
                if head and 1 <= step <= HEADS:
                    head_wh(hb, step - 1, hi)

            def sum_to_den(c):
                dve.tensor_scalar(row_den[:, c:c + 1], row_sum[:, c:c + 1], TINY, None, ALU.max) \
                    .then_inc(S["den_ready"], 1)

            for j in range(HEADS):
                head_stats(0, j, 0, 1)
                head_mean_var(0, j, False)
                head_wh(0, j, 0)
            for u in range(-5, 0):
                slot(0, u, PAIRS == 1)
            if PAIRS > 1:
                with dve.Fori(0, PAIRS - 1) as k:
                    for u in range(UT):
                        slot(k, u, False)
            for u in range(UT):
                slot(PAIRS - 1, u, True)


def gate_block(nc, B, Wo, ident, minus_half, node_table, wr_sb, br_sb, bo_sb, bn_rows, w_bc, wo_hi, wo_lo,
               bn_scale, bn_shift):
    TB, D = node_table.shape[1], node_table.shape[2]
    E, KB = wr_sb.shape[2], D // P
    CT = BANK // P
    EK = E * KB

    ctx = ExitStack()
    with ctx:
        def sb(name, shape, dt=FP32):
            return ctx.enter_context(nc.sbuf_tensor(f"gate_{name}", shape, dt))

        featT = sb("featT", [P, TB * KB, P])
        logits, expd, w_sb = (sb(n, [P, TB, E]) for n in ("logits", "expd", "w_sb"))
        top, total, inv = (sb(n, [P, TB]) for n in ("top", "total", "inv"))
        wT_sb = sb("wT_sb", [E, TB * P])
        bn_cols = [sb(f"bn_cols{i}", [P, 5, EK]) for i in range(2)]
        bn_eps, bn_rsqrt, bn_diff = (sb(n, [P, 2, EK]) for n in ("bn_eps", "bn_rsqrt", "bn_diff"))
        wo_stage = sb("wo_stage", [P, E, KB * D])
        banks = [ctx.enter_context(nc.psum_tensor(f"gate_ps{i}", [P, 2, BANK], FP32)) for i in range(4)]

        wo_in = [ctx.enter_context(nc.semaphore(f"wo_in{i}")) for i in range(2)]
        names = """featT_psum featT_ready logits_psum logits_ready top_ready centred_ready exp_ready total_ready
            inv_ready w_ready wT_psum wT_ready table_psum table_ready spread_psum spread_ready
            bn_psum bn_cols_ready bn_eps_ready bn_rsqrt_ready bn_scale_ready bn_diff_ready bn_prod_ready
            wo_hi_ready""".split()
        S = {n: ctx.enter_context(nc.semaphore(f"gate_{n}")) for n in names}

        block = ctx.enter_context(nc.Block())

        @block.sync
        def _(sp):
            for i in range(2):
                h = slice(i * E // 2, (i + 1) * E // 2)
                sp.dma_start(wo_stage[:, h, :].rearrange("p e (k d) -> p e k d", k=KB),
                             Wo[h].rearrange("e (k p) d -> p e k d", p=P)).then_inc(wo_in[i], DMA)

        @block.tensor
        def _(pe):
            for it in range(TB):
                for d in range(KB):
                    i = it * KB + d
                    last = pe.transpose(banks[i // 8][:, (i % 8) // 4, (i % 4) * P:(i % 4 + 1) * P],
                                        node_table[:, it, d * P:(d + 1) * P], ident[:, :])
            last.then_inc(S["featT_psum"], 1)
            for i in range(2):
                last = pe.transpose(banks[3][:, i, 0:5 * EK], bn_rows[i][:, :], ident[0:5 * EK, 0:5 * EK])
            last.then_inc(S["bn_psum"], 1)
            pe.wait_ge(S["featT_ready"], 1)
            for it in range(TB):
                for d in range(KB):
                    last = pe.matmul(banks[2][:, 0, it * E:(it + 1) * E], featT[:, it * KB + d, :], wr_sb[:, d, :],
                                     start=(d == 0), stop=(d == KB - 1))
            last.then_inc(S["logits_psum"], 1)
            pe.wait_ge(S["w_ready"], 1)
            for it in range(TB):
                last = pe.transpose(banks[2][0:E, it // CT, (it % CT) * P:(it % CT + 1) * P], w_sb[:, it, :], ident[:, :])
            last.then_inc(S["wT_psum"], 1)
            pe.wait_ge(S["wT_ready"], 1)
            for it in range(TB):
                last = pe.matmul(banks[it // 4][:, (it % 4) // 2, (it % 2) * D:(it % 2 + 1) * D],
                                 wT_sb[:, it * P:(it + 1) * P], bo_sb[:, :], start=True, stop=True)
            last.then_inc(S["table_psum"], 1)
            for e in range(E):
                if e == 0:
                    pe.wait_ge(S["bn_cols_ready"], 1)
                elif e == 1:
                    pass
                elif e == 2:
                    pe.wait_ge(S["table_ready"], 1)
                else:
                    pe.wait_ge(S["spread_ready"], e - 3)
                pair = banks[(3, 2, 0, 1)[e % 4]]
                if e >= 4:
                    pe.wait_ge(S["spread_ready"], e - 3)
                for it in range(TB):
                    last = pe.transpose(pair[:, it // CT, (it % CT) * P:(it % CT + 1) * P],
                                        w_sb[:, it, e:e + 1].to_broadcast([P, P]), ident[:, :])
                last.then_inc(S["spread_psum"], 1)

        @block.scalar
        def _(act):
            act.wait_ge(S["featT_psum"], 1)
            for i in range(2):
                last = act.activation(featT[:, i * 8:(i + 1) * 8, :].rearrange("p i c -> p (i c)"),
                                      banks[i][:, :, :].rearrange("p k c -> p (k c)"), ACT.Copy, scale=1.0 / B)
            last.then_inc(S["featT_ready"], 1)
            act.wait_ge(S["centred_ready"], 1)
            act.activation(expd[:, :, :], logits[:, :, :], ACT.Exp).then_inc(S["exp_ready"], 1)
            act.wait_ge(S["wT_psum"], 1)
            act.activation(wT_sb[:, :], banks[2][0:E, :, :].rearrange("e k c -> e (k c)"), ACT.Copy) \
                .then_inc(S["wT_ready"], 1)
            for e in range(E):
                act.wait_ge(S["spread_psum"], e + 1)
                pair = banks[(3, 2, 0, 1)[e % 4]]
                act.activation(w_bc[:, :, e, :], pair[:, :, :], ACT.Copy).then_inc(S["spread_ready"], 1)

        @block.gpsimd
        def _(pool):
            pool.wait_ge(S["bn_eps_ready"], 1)
            pool.tensor_tensor(bn_rsqrt[:, :, :].rearrange("p i c -> p (i c)"),
                               bn_eps[:, :, :].rearrange("p i c -> p (i c)"),
                               minus_half[:, 0:1].to_broadcast([P, 2 * EK]), ALU.pow).then_inc(S["bn_rsqrt_ready"], 1)

        @block.vector
        def _(dve):
            dve.wait_ge(S["bn_psum"], 1)
            for i in range(2):
                last = dve.tensor_copy(bn_cols[i][:, :, :].rearrange("p i c -> p (i c)"), banks[3][:, i, 0:5 * EK])
            last.then_inc(S["bn_cols_ready"], 1)
            dve.wait_ge(S["bn_cols_ready"], 1)
            BIAS, GAMMA, BETA, MEAN, VAR = range(5)
            for i in range(2):
                last = dve.tensor_scalar(bn_eps[:, i, :], bn_cols[i][:, VAR, :], BN_EPS, None, ALU.add)
            last.then_inc(S["bn_eps_ready"], 1)
            dve.wait_ge(S["logits_psum"], 1)
            dve.tensor_tensor(expd[:, :, :], banks[2][:, 0, 0:TB * E].rearrange("p (t e) -> p t e", e=E),
                              br_sb[:, :].unsqueeze(1).to_broadcast([P, TB, E]), ALU.add).then_inc(S["logits_ready"], 1)
            dve.wait_ge(S["logits_ready"], 1)
            dve.tensor_reduce(top[:, :], expd[:, :, :], AX.X, ALU.max).then_inc(S["top_ready"], 1)
            dve.wait_ge(S["top_ready"], 1)
            dve.tensor_tensor(logits[:, :, :], expd[:, :, :], top[:, :].unsqueeze(2).to_broadcast([P, TB, E]),
                              ALU.subtract).then_inc(S["centred_ready"], 1)
            dve.wait_ge(S["exp_ready"], 1)
            dve.tensor_reduce(total[:, :], expd[:, :, :], AX.X, ALU.add).then_inc(S["total_ready"], 1)
            dve.wait_ge(S["total_ready"], 1)
            dve.reciprocal(inv[:, :], total[:, :]).then_inc(S["inv_ready"], 1)
            dve.wait_ge(S["inv_ready"], 1)
            dve.tensor_tensor(w_sb[:, :, :], expd[:, :, :], inv[:, :].unsqueeze(2).to_broadcast([P, TB, E]),
                              ALU.mult).then_inc(S["w_ready"], 1)
            dve.wait_ge(S["bn_rsqrt_ready"], 1)
            for i in range(2):
                dve.tensor_tensor(bn_scale[i][:, :], bn_rsqrt[:, i, :], bn_cols[i][:, GAMMA, :], ALU.mult) \
                    .then_inc(S["bn_scale_ready"], 1)
                dve.tensor_tensor(bn_diff[:, i, :], bn_cols[i][:, BIAS, :], bn_cols[i][:, MEAN, :], ALU.subtract) \
                    .then_inc(S["bn_diff_ready"], 1)
            for i in range(2):
                dve.wait_ge(S["bn_scale_ready"], i + 1)
                dve.wait_ge(S["bn_diff_ready"], i + 1)
                dve.tensor_tensor(bn_eps[:, i, :], bn_diff[:, i, :], bn_scale[i][:, :], ALU.mult) \
                    .then_inc(S["bn_prod_ready"], 1)
            for i in range(2):
                dve.wait_ge(S["bn_prod_ready"], i + 1)
                dve.tensor_tensor(bn_shift[i][:, :], bn_eps[:, i, :], bn_cols[i][:, BETA, :], ALU.add)
            for i in range(2):
                h = slice(i * E // 2, (i + 1) * E // 2)
                dve.wait_ge(wo_in[i], DMA)
                dve.tensor_copy(wo_hi[:, h, :], wo_stage[:, h, :]).then_inc(S["wo_hi_ready"], 1)
            dve.wait_ge(S["table_psum"], 1)
            for i in range(2):
                last = dve.tensor_copy(node_table[:, i * CT:(i + 1) * CT, :].rearrange("p t d -> p (t d)"),
                                       banks[i][:, :, :].rearrange("p k c -> p (k c)"))
            last.then_inc(S["table_ready"], 1)
            for i in range(2):
                h = slice(i * E // 2, (i + 1) * E // 2)
                dve.wait_ge(S["wo_hi_ready"], i + 1)
                dve.tensor_tensor(wo_lo[:, h, :], wo_stage[:, h, :], bits(wo_hi[:, h, :]), ALU.subtract)


def ffn_block(nc, B, x1_dram, out, ident, minus_half, ln_eps, w_bo, w12_hi, w12_lo, wo_hi, wo_lo, w_bc, bn_scale, bn_shift):
    D = w_bo.shape[2]
    KB, E, CT = D // P, w_bc.shape[2], BANK // P
    CH = w_bc.shape[1]
    US = CH * E
    LOOK = 3

    ctx = ExitStack()
    with ctx:
        def sb(name, shape, dt=FP32):
            return ctx.enter_context(nc.sbuf_tensor(name, shape, dt))

        def ps(name):
            return ctx.enter_context(nc.psum_tensor(name, [P, KB, BANK], FP32))

        def sem(name):
            return ctx.enter_context(nc.semaphore(name))

        x1_sb = [sb(f"ffn_x1{i}", [P, CT, D]) for i in range(2)]
        xn_sb = sb("ffn_xn", [P, CT, D])
        stats, mv = sb("ffn_stats", [P, CT, 6]), sb("ffn_mv", [P, CT, 2])
        vareps, rstd = sb("ffn_vareps", [P, CT]), sb("ffn_rstd", [P, CT])
        xT_hi, xT_lo = sb("xT_hi", [P, KB, BANK], FP32R), sb("xT_lo", [P, KB, BANK], FP32R)
        h1 = sb("h1", [P, KB, BANK])
        h1_hi = [sb(f"h1_hi{i}", [P, KB, BANK], FP32R) for i in range(2)]
        h1_lo = [sb(f"h1_lo{i}", [P, KB, BANK], FP32R) for i in range(2)]
        h2 = sb("h2", [P, KB, BANK])
        h2_hi = [sb(f"h2_hi{i}", [P, KB, BANK], FP32R) for i in range(2)]
        h2_lo = [sb(f"h2_lo{i}", [P, KB, BANK], FP32R) for i in range(2)]
        yT_sb = sb("yT_sb", [P, KB, BANK])

        z1_ps, z2_ps, y_ps, turn_ps = ps("z1_ps"), ps("z2_ps"), ps("y_ps"), ps("turn_ps")

        x1_in = [sem(f"ffn_x1_in{i}") for i in range(2)]
        stored = [sem(f"ffn_stored{i}") for i in range(2)]
        names = """stat mv_ready vareps_ready rstd_ready xn_ready residual_ready xT_psum xT_hi_ready xT_lo_ready
            z1_ready h1_ready h1_hi_ready h1_lo_ready z2_ready relu2_ready gated_ready h2_hi_ready h2_lo_ready
            step_done yT_ready out_psum out_ready""".split()
        S = {n: sem(f"ffn_{n}") for n in names}

        def step_at(b, u, off, last):
            t = u + off
            ok = t >= 0 and (t < US or not last)
            return ok, (t // E) % CH, t % E, b * US + (t + 1)

        def next_tile(b, u, last):
            t = u // E + 1
            return t >= 1 and (t < CH or not last), t % CH, b * CH + (t + 1)

        block = ctx.enter_context(nc.Block())

        @block.sync
        def _(sp):
            def load(b, c):
                sp.dma_start(x1_sb[c][:, :, :], x1_dram[c, b]).then_inc(x1_in[c], DMA)

            def store(b, c, last):
                wait(sp, S["out_ready"], b * CH + (c + 1))
                sp.dma_start(out[b].rearrange("(c s p) d -> c p s d", c=CH, p=P)[c], x1_sb[c][:, :, :]) \
                    .then_inc(stored[c], DMA)
                if not last:
                    sp.wait_ge(stored[c], DMA * (b + 1))
                    load(b + 1, c)

            for c in range(CH):
                load(0, c)
            if B > 1:
                with sp.Fori(0, B - 1) as b:
                    for c in range(CH):
                        store(b, c, False)
            for c in range(CH):
                store(B - 1, c, True)
            for c in range(CH):
                sp.wait_ge(stored[c], DMA * B)

        @block.gpsimd
        def _(pool):
            def tile(b, c):
                n = b * CH + (c + 1)
                pool.wait_ge(S["mv_ready"], n)
                pool.tensor_tensor(vareps[:, :], mv[:, :, 1], ln_eps[:, 0:CT], ALU.add).then_inc(S["vareps_ready"], 1)
                pool.wait_ge(S["vareps_ready"], n)
                pool.tensor_tensor(rstd[:, :], vareps[:, :], minus_half[:, 0:CT], ALU.pow).then_inc(S["rstd_ready"], 1)
                pool.wait_ge(S["xn_ready"], n)
                pool.tensor_tensor(x1_sb[c][:, :, :], x1_sb[c][:, :, :], w_bo[:, c * CT:(c + 1) * CT, :], ALU.add) \
                    .then_inc(S["residual_ready"], 1)

            if B > 1:
                with pool.Fori(0, B - 1) as b:
                    for c in range(CH):
                        tile(b, c)
            for c in range(CH):
                tile(B - 1, c)

        @block.tensor
        def _(pe):
            def transpose_x(n):
                pe.wait_ge(S["xn_ready"], n)
                wait(pe, S["out_ready"], n - 2)
                for d in range(KB):
                    for s in range(CT):
                        last = pe.transpose(turn_ps[:, d, s * P:(s + 1) * P], xn_sb[:, s, d * P:(d + 1) * P], ident[:, :])
                last.then_inc(S["xT_psum"], 1)

            def transpose_y(n):
                pe.wait_ge(S["yT_ready"], n)
                for s in range(CT):
                    for d in range(KB):
                        at = (s % 2) * D + d * P
                        last = pe.transpose(turn_ps[:, s // 2, at:at + P], yT_sb[:, d, s * P:(s + 1) * P], ident[:, :])
                last.then_inc(S["out_psum"], 1)

            def layer(acc, w_hi, w_lo, x_hi, x_lo, first, last):
                for m in range(KB):
                    for k in range(KB):
                        at = slice(k * D + m * P, k * D + (m + 1) * P)
                        done = split_matmul(pe, acc[:, m, :], w_hi[:, at], w_lo[:, at], x_hi[:, k, :], x_lo[:, k, :],
                                            first and k == 0, last and k == KB - 1)
                return done

            def slot(b, u, last):
                ok, c, e, n = step_at(b, u, 3, last)
                if ok:
                    if e == 0:
                        pe.wait_ge(S["xT_lo_ready"], b * CH + ((u + 3) // E + 1))
                    wait(pe, S["h1_ready"], n - 1)
                    layer(z1_ps, w12_hi[:, 0, e, :], w12_lo[:, 0, e, :], xT_hi, xT_lo, True, True) \
                        .then_inc(S["z1_ready"], 1)
                ok, _, n = next_tile(b, u, last)
                if ok and u % E == 4:
                    transpose_x(n)
                if u >= 0 and u % E == E - 1:
                    transpose_y(b * CH + (u // E + 1))
                ok, c, e, n = step_at(b, u, 2, last)
                if ok:
                    pe.wait_ge(S["h1_lo_ready"], n)
                    wait(pe, S["relu2_ready"], n - 1)
                    layer(z2_ps, w12_hi[:, 1, e, :], w12_lo[:, 1, e, :], h1_hi[n_par(u + 2)], h1_lo[n_par(u + 2)],
                          True, True).then_inc(S["z2_ready"], 1)
                ok, c, e, n = step_at(b, u, 1, last)
                if ok:
                    pe.wait_ge(S["h2_lo_ready"], n)
                    if e == 0:
                        wait(pe, S["yT_ready"], b * CH + (u + 1) // E)
                    layer(y_ps, wo_hi[:, e, :], wo_lo[:, e, :], h2_hi[n_par(u + 1)], h2_lo[n_par(u + 1)],
                          e == 0, e == E - 1).then_inc(S["step_done"], 1)

            transpose_x(1)
            for u in range(-LOOK, 0):
                slot(0, u, B == 1)
            if B > 1:
                with pe.Fori(0, B - 1) as b:
                    for u in range(US):
                        slot(b, u, False)
            for u in range(US):
                slot(B - 1, u, True)

        @block.scalar
        def _(act):
            def split_x(n):
                act.wait_ge(S["xT_psum"], n)
                act.activation(xT_hi[:, :, :], turn_ps[:, :, :], ACT.Copy).then_inc(S["xT_hi_ready"], 1)

            def bn_relu(dst, src, layer, e, m):
                col = slice(e * KB + m, e * KB + m + 1)
                return act.activation(dst[:, m, :], src[:, m, :], ACT.Relu, bias=bn_shift[layer][:, col],
                                      scale=bn_scale[layer][:, col])

            def slot(b, u, last):
                if u >= 0 and u % E == E - 1:
                    act.wait_ge(S["step_done"], b * US + (u + 1))
                    act.activation(yT_sb[:, :, :], y_ps[:, :, :], ACT.Copy).then_inc(S["yT_ready"], 1)
                ok, c, e, n = step_at(b, u, 3, last)
                if ok:
                    act.wait_ge(S["z1_ready"], n)
                    wait(act, S["h1_lo_ready"], n - 1)
                    for m in range(KB):
                        done = bn_relu(h1, z1_ps, 0, e, m)
                    done.then_inc(S["h1_ready"], 1)
                    act.wait_ge(S["h1_ready"], n)
                    wait(act, S["z2_ready"], n - 2)
                    act.activation(h1_hi[n_par(u + 3)][:, :, :], h1[:, :, :], ACT.Copy).then_inc(S["h1_hi_ready"], 1)
                ok, _, n = next_tile(b, u, last)
                if ok and u % E == 4:
                    act.wait_ge(S["z1_ready"], b * US + (u + 3 + 1))
                    split_x(n)
                ok, c, e, n = step_at(b, u, 2, last)
                if ok:
                    act.wait_ge(S["z2_ready"], n)
                    wait(act, S["h2_lo_ready"], n - 1)
                    for m in range(KB):
                        done = bn_relu(h2, z2_ps, 1, e, m)
                    done.then_inc(S["relu2_ready"], 1)

            split_x(1)
            for u in range(-LOOK, 0):
                slot(0, u, B == 1)
            if B > 1:
                with act.Fori(0, B - 1) as b:
                    for u in range(US):
                        slot(b, u, False)
            for u in range(US):
                slot(B - 1, u, True)

        @block.vector
        def _(dve):
            def statistics(c, n, turn):
                dve.wait_ge(x1_in[c], DMA * turn)
                for s in range(CT):
                    dve.bn_stats(stats[:, s, :], x1_sb[c][:, s, :]).then_inc(S["stat"], 1)

            def mean_var(n, waited):
                if not waited:
                    dve.wait_ge(S["stat"], CT * n)
                for s in range(CT):
                    last = dve.bn_aggr(mv[:, s, :], stats[:, s, :])
                last.then_inc(S["mv_ready"], 1)

            def normalise(c, n):
                dve.wait_ge(S["rstd_ready"], n)
                for s in range(CT):
                    last = dve.tensor_scalar(xn_sb[:, s, :], x1_sb[c][:, s, :], mv[:, s, 0:1], rstd[:, s:s + 1],
                                             ALU.subtract, ALU.mult)
                last.then_inc(S["xn_ready"], 1)

            def split_x(n):
                dve.wait_ge(S["xT_hi_ready"], n)
                dve.tensor_tensor(xT_lo[:, :, :], turn_ps[:, :, :], bits(xT_hi[:, :, :]), ALU.subtract) \
                    .then_inc(S["xT_lo_ready"], 1)

            def slot(b, u, last):
                tile_ok, tc, tn = next_tile(b, u, last)
                ok, c, e, n = step_at(b, u, 3, last)
                if ok:
                    i = n_par(u + 3)
                    if tile_ok and u % E == 3:
                        dve.wait_ge(S["stat"], CT * tn)
                    dve.wait_ge(S["h1_hi_ready"], n)
                    dve.tensor_tensor(h1_lo[i][:, :, :], h1[:, :, :], bits(h1_hi[i][:, :, :]), ALU.subtract) \
                        .then_inc(S["h1_lo_ready"], 1)
                if tile_ok and u % E == 3:
                    mean_var(tn, ok)
                if tile_ok and u % E == 4:
                    split_x(tn)
                ok, c, e, n = step_at(b, u, 2, last)
                if ok:
                    i = n_par(u + 2)
                    dve.wait_ge(S["relu2_ready"], n)
                    dve.tensor_tensor(h2[:, :, :], h2[:, :, :], w_bc[:, c, e, :].unsqueeze(1).to_broadcast([P, KB, BANK]),
                                      ALU.mult).then_inc(S["gated_ready"], 1)
                    dve.wait_ge(S["gated_ready"], n)
                    wait(dve, S["step_done"], n - 2)
                    dve.tensor_copy(h2_hi[i][:, :, :], h2[:, :, :]).then_inc(S["h2_hi_ready"], 1)
                    dve.wait_ge(S["h2_hi_ready"], n)
                    dve.tensor_tensor(h2_lo[i][:, :, :], h2[:, :, :], bits(h2_hi[i][:, :, :]), ALU.subtract) \
                        .then_inc(S["h2_lo_ready"], 1)
                if u >= 0 and u % E == E - 1:
                    t = u // E
                    dve.wait_ge(S["out_psum"], b * CH + (t + 1))
                    dve.wait_ge(S["residual_ready"], b * CH + (t + 1))
                    rows = x1_sb[t][:, :, :].rearrange("p s d -> p (s d)")
                    dve.tensor_tensor(rows, turn_ps[:, :, :].rearrange("p k c -> p (k c)"), rows, ALU.add) \
                        .then_inc(S["out_ready"], 1)
                if tile_ok and u % E == 2:
                    statistics(tc, tn, b + (u // E + 1) // CH + 1)
                if tile_ok and u % E == 3:
                    normalise(tc, tn)

            statistics(0, 1, 1)
            mean_var(1, False)
            normalise(0, 1)
            split_x(1)
            for u in range(-LOOK, 0):
                slot(0, u, B == 1)
            if B > 1:
                with dve.Fori(0, B - 1) as b:
                    for u in range(US):
                        slot(b, u, False)
            for u in range(US):
                slot(B - 1, u, True)


def n_par(t):
    return t % 2


INPUTS = ["x", "adj", "L0_gnn_W", "L0_gnn_a", "L0_ffn_Wr", "L0_ffn_br",
          "L0_ffn_W1", "L0_ffn_b1", "L0_ffn_g1", "L0_ffn_be1", "L0_ffn_m1", "L0_ffn_v1",
          "L0_ffn_W2", "L0_ffn_b2", "L0_ffn_g2", "L0_ffn_be2", "L0_ffn_m2", "L0_ffn_v2", "L0_ffn_Wo", "L0_ffn_bo"]


def kernel(**inputs):
    import numpy as np
    import concourse.bacc as bacc
    from concourse.bass_utils import run_bass_kernel_spmd

    nc = bacc.Bacc("TRN2", target_bir_lowering=False, num_devices=1)
    arrays, args = {}, []
    for name in INPUTS:
        array = np.ascontiguousarray(inputs[name])
        arrays[f"in_{name}"] = array
        args.append(nc.dram_tensor(f"in_{name}", array.shape, mybir.dt.from_np(array.dtype), kind="ExternalInput").ap())
    args.append(nc.dram_tensor("out", arrays["in_x"].shape, FP32, kind="ExternalOutput").ap())
    program(nc, *args)
    result = run_bass_kernel_spmd(nc, [arrays], core_ids=[0])
    return result.results[0]["out"]
```

```python
from contextlib import ExitStack

import concourse.bass as bass
import concourse.mybir as mybir

FP32 = mybir.dt.float32
FP32R = mybir.dt.float32r
INT32 = mybir.dt.int32
ALU = mybir.AluOpType
ACT = mybir.ActivationFunctionType
AX = mybir.AxisListType

P = 128
BANK = 512
LN_EPS = 1e-5
BN_EPS = 1e-3
SLOPE = 0.2
EDGE_UNIT = 2.0 ** -64
TINY = 1e-30
DMA = 16


def wait(eng, sem, value):
    if isinstance(value, int) and value <= 0:
        return
    eng.wait_ge(sem, value)


def bits(ap):
    return ap.bitcast(FP32)


def split_matmul(pe, out, w_hi, w_lo, x_hi, x_lo, first, last):
    pe.matmul(out, w_hi, x_hi, start=first, stop=False)
    pe.matmul(out, w_hi, x_lo, start=False, stop=False)
    return pe.matmul(out, w_lo, x_hi, start=False, stop=last)


class TileNorm:

    def __init__(self, keep, sem, minus_half, ln_eps, CT, D):
        self.CT, self.minus_half, self.ln_eps = CT, minus_half, ln_eps
        self.xn = keep("ffn_xn", [P, CT, D])
        self.stats, self.mv = keep("ffn_stats", [P, CT, 6]), keep("ffn_mv", [P, CT, 2])
        self.vareps, self.rstd = keep("ffn_vareps", [P, CT]), keep("ffn_rstd", [P, CT])
        self.stat, self.mv_ready, self.vareps_ready = sem("ffn_stat"), sem("ffn_mv_ready"), sem("ffn_vareps_ready")
        self.rstd_ready, self.xn_ready = sem("ffn_rstd_ready"), sem("ffn_xn_ready")

    def statistics(self, dve, x1, x1_in, turn):
        dve.wait_ge(x1_in, DMA * turn)
        for s in range(self.CT):
            dve.bn_stats(self.stats[:, s, :], x1[:, s, :]).then_inc(self.stat, 1)

    def mean_var(self, dve, n, waited):
        if not waited:
            dve.wait_ge(self.stat, self.CT * n)
        for s in range(self.CT):
            last = dve.bn_aggr(self.mv[:, s, :], self.stats[:, s, :])
        last.then_inc(self.mv_ready, 1)

    def deviation(self, pool, n):
        pool.wait_ge(self.mv_ready, n)
        pool.tensor_tensor(self.vareps[:, :], self.mv[:, :, 1], self.ln_eps[:, :], ALU.add) \
            .then_inc(self.vareps_ready, 1)
        pool.wait_ge(self.vareps_ready, n)
        pool.tensor_tensor(self.rstd[:, :], self.vareps[:, :], self.minus_half[:, :], ALU.pow) \
            .then_inc(self.rstd_ready, 1)

    def normalise(self, dve, x1, n):
        dve.wait_ge(self.rstd_ready, n)
        for s in range(self.CT):
            last = dve.tensor_scalar(self.xn[:, s, :], x1[:, s, :], self.mv[:, s, 0:1], self.rstd[:, s:s + 1],
                                     ALU.subtract, ALU.mult)
        last.then_inc(self.xn_ready, 1)


def program(nc, x, adj, W, a, Wr, br, W1, b1, g1, be1, m1, v1, W2, b2, g2, be2, m2, v2, Wo, bo, out):
    B, N, D = x.shape
    E = Wr.shape[1]
    KB = D // P
    TB = N // P
    CT = BANK // P
    CH = N // BANK
    assert B % 2 == 0 and D == 2 * P and CH == 2 and E == 8 and TB == 8

    x1_dram = nc.dram_tensor("x1_scratch", [CH, B, P, CT, D], FP32, kind="Internal").ap()
    w_dram = nc.dram_tensor("w_scratch", [E, CH, BANK], FP32, kind="Internal").ap()

    persistent = ExitStack()
    with persistent:
        def keep(name, shape, dt=FP32):
            return persistent.enter_context(nc.sbuf_tensor(name, shape, dt))

        ident = keep("ident", [P, P])
        minus_half, ln_eps = keep("minus_half", [P, CT]), keep("ln_eps", [P, CT])
        w12_hi = keep("w12_hi", [P, 2, E, KB * D], FP32R)
        w12_lo = keep("w12_lo", [P, 2, E, KB * D], FP32R)
        node_table = keep("node_table", [P, TB, D])
        wr_sb = keep("wr_sb", [P, KB, E])
        br_sb = keep("br_sb", [P, E])
        bo_sb = keep("bo_sb", [E, D])
        bn_scale = [keep(f"bn_scale{i}", [P, E * KB]) for i in range(2)]
        bn_shift = [keep(f"bn_shift{i}", [P, E * KB]) for i in range(2)]

        def keep_sem(name):
            return persistent.enter_context(nc.semaphore(name))

        norm = TileNorm(keep, keep_sem, minus_half, ln_eps, CT, D)
        ffn_x1, ffn_x1_in = keep("ffn_x10", [P, CT, D]), keep_sem("ffn_x1_in0")

        attention_block(nc, x, adj, W, a, W1, W2, x1_dram, ident, minus_half, ln_eps, w12_hi, w12_lo, node_table,
                        (Wr, br, bo, (b1, g1, be1, m1, v1), (b2, g2, be2, m2, v2)),
                        (wr_sb, br_sb, bo_sb, bn_scale, bn_shift), norm, ffn_x1, ffn_x1_in)

        ffn_block(nc, B, Wo, x1_dram, w_dram, out, ident, minus_half, node_table, w12_hi, w12_lo,
                  wr_sb, br_sb, bo_sb, bn_scale, bn_shift, norm, ffn_x1, ffn_x1_in)


def attention_block(nc, x, adj, W, a, W1, W2, x1_dram, ident, minus_half, ln_eps, w12_hi, w12_lo, feat_sum,
                    small_dram, small_sb, norm, ffn_x1, ffn_x1_in):
    B, N, D = x.shape
    E = W1.shape[0]
    KB, TB, CT = D // P, N // P, BANK // P
    PAIRS = B // 2
    UT = 2 * TB
    DX = D + 2
    HEADS = TB // 2
    Wr, br, bo, bn1, bn2 = small_dram
    wr_sb, br_sb, bo_sb, bn_scale, bn_shift = small_sb
    EK = E * KB
    NORM_SLOT = UT - 7
    EP = E // PAIRS
    TASKS = 2 * EP
    TASK_SLOTS = UT // TASKS
    assert E % PAIRS == 0 and UT % TASKS == 0

    ctx = ExitStack()
    with ctx:
        def sb(name, shape, dt=FP32):
            return ctx.enter_context(nc.sbuf_tensor(name, shape, dt))

        def ps(name, shape, dt=FP32):
            return ctx.enter_context(nc.psum_tensor(name, shape, dt))

        def sem(name):
            return ctx.enter_context(nc.semaphore(name))

        w_sb = sb("w_sb", [P, KB, D])
        a_sb = sb("a_sb", [P, KB, 2])
        wx = sb("wx", [P, KB, DX])
        x_sb = [sb(f"x_sb{i}", [P, TB, D]) for i in range(2)]
        adj_sb = [sb(f"adj_sb{i}", [P, N], INT32) for i in range(2)]
        ej_rows = [sb(f"ej_rows{i}", [P, N]) for i in range(2)]
        scores = [sb(f"scores{i}", [P, N]) for i in range(4)]
        upper = [sb(f"upper{i}", [P, N]) for i in range(2)]
        pT_hi = [sb(f"pT_hi{i}", [P, TB, P], FP32R) for i in range(2)]
        pT_lo = [sb(f"pT_lo{i}", [P, TB, P], FP32R) for i in range(2)]
        wh_hi = [sb(f"wh_hi{i}", [P, TB, D], FP32R) for i in range(2)]
        wh_lo = [sb(f"wh_lo{i}", [P, TB, D], FP32R) for i in range(2)]
        e_cols = [sb(f"e_cols{i}", [P, TB, 2]) for i in range(2)]
        row_max, neg_max = (sb(n, [P, 4]) for n in ("row_max", "neg_max"))
        tiny = sb("tiny", [P, 1])
        row_sum, row_den, row_inv = (sb(n, [P, 4]) for n in ("row_sum", "row_den", "row_inv"))
        x1_sb = [sb(f"x1_sb{i}", [P, D]) for i in range(4)]
        x1_sum, x1_mean, x1_squares = (sb(n, [P, 4]) for n in ("x1_sum", "x1_mean", "x1_squares"))
        x1_deviation = w_sb[:, 0, :]
        x1_vareps, x1_rstd = sb("x1_vareps", [P, 4]), sb("x1_rstd", [P, 4])
        sum_eps = sb("sum_eps", [P, 1])
        n1_sb = [sb(f"n1_sb{i}", [P, D]) for i in range(2)]
        xs_stats, xs_mv = sb("xs_stats", [P, 2, 2, 6]), sb("xs_mv", [P, 2, 2, 2])
        xs_vareps, xs_rstd = sb("xs_vareps", [P, 2, 2]), sb("xs_rstd", [P, 2, 2])
        w_stats, w_mv, w_centred = sb("w_stats", [P, KB, 6]), sb("w_mv", [P, KB, 2]), sb("w_centred", [P, KB, D])
        bn_rows = [sb(f"bn_rows{i}", [5 * EK, P]) for i in range(2)]
        bn_cols = [sb(f"bn_cols{i}", [P, 5, EK]) for i in range(2)]
        bn_eps, bn_rsqrt, bn_diff = (sb(n, [P, 2, EK]) for n in ("bn_eps", "bn_rsqrt", "bn_diff"))
        hT = sb("hT", [P, KB, 2 * P])
        w_stage = [sb(f"w_stage{i}", [P, KB * D]) for i in range(2)]

        pT_ps = [ps(f"pT_ps{i}", [P, TB, P]) for i in range(2)]
        attn_ps = ps("attn_ps", [P, 2, BANK])
        head_ps = ps("head_ps", [P, 2, BANK])

        small_in = sem("small_in")
        w_in = sem("w_in")
        x_in = [[sem(f"x_in{i}{j}") for j in range(HEADS)] for i in range(2)]
        adj_in = [sem(f"adj_in{i}") for i in range(2)]
        stage_in = [sem(f"w_stage_in{i}") for i in range(2)]
        x1_stored = [sem(f"x1_stored{i}") for i in range(4)]
        names = """const_zero const_ready w_stat w_mv_ready w_centred_ready a_scaled wT_ready wx_ready
            xs_stat xs_mv_ready xs_vareps_ready xs_rstd_ready hT_psum hT_ready
            wh_ready wh_hi_ready wh_lo_ready ej_rows_psum ej_rows_ready
            masked_ready upper_ready lrelu_ready negmax_ready probs_ready
            pT_ready pT_hi_ready pT_lo_ready attn_ready den_ready inv_ready x1_ready
            x1_mean_ready x1_squares_ready x1_vareps_ready x1_rstd_ready n1_ready n1_added
            w12_hi_ready w12_lo_ready bn_psum bn_cols_ready bn_eps_ready bn_rsqrt_ready
            bn_scale_ready bn_diff_ready bn_prod_ready""".split()
        S = {n: sem(n) for n in names}

        def tile_at(k, u, off, last):
            t = u + off
            ok = (t >= 0 or not isinstance(k, int)) and (t < UT or not last)
            return ok, t, k * UT + (t + 1)

        def head_at(k, u, last):
            g = u + 3
            if g < 0:
                return None
            off = g // TB + 1
            return None if last and off >= 2 else (off, g % TB)

        def task_at(k, i):
            return i // EP, k * EP + i % EP

        def first_head(j):
            return (pT_ps[j // 2][:, (j % 2) * 2 * KB:(j % 2 + 1) * 2 * KB, :].rearrange("p t c -> p (t c)"),
                    upper[j // 2][:, (j % 2) * BANK:(j % 2 + 1) * BANK].rearrange("p (k c) -> p k c", k=KB),
                    (head_ps, attn_ps)[j % 2])

        def later_head(j):
            return head_ps[:, 0, :], hT[:, :, :], head_ps

        def parity(t):
            return (t // TB) % 2

        block = ctx.enter_context(nc.Block())

        @block.sync
        def _(sp):
            sp.dma_start(w_sb[:, :, :], W.rearrange("(o p) d -> p o d", p=P)).then_inc(w_in, DMA)
            for h in range(2):
                sp.dma_start(a_sb[:, :, h], a.rearrange("(h o p) -> h p o", p=P, o=KB)[h],
                             allow_slow_non_contiguous=True).then_inc(w_in, DMA)

            def load_x(b, i, j):
                h = slice(2 * j, 2 * j + 2)
                sp.dma_start(x_sb[i][:, h, :], x[b].rearrange("(t p) d -> p t d", p=P)[:, h, :]) \
                    .then_inc(x_in[i][j], DMA)

            def load_adj(b, it, i):
                sp.dma_start(adj_sb[i][:, :], adj[b, it * P:(it + 1) * P, :]).then_inc(adj_in[i], DMA)

            for j in range(HEADS):
                load_x(0, 0, j)
            load_adj(0, 0, 0)
            load_adj(0, 1, 1)
            for j in range(HEADS):
                load_x(1, 1, j)
            sp.dma_start(wr_sb[:, :, :], Wr.rearrange("(k p) e -> p k e", p=P),
                         allow_slow_non_contiguous=True).then_inc(small_in, DMA)
            sp.dma_start(br_sb[:, :], br.partition_broadcast(P)).then_inc(small_in, DMA)
            sp.dma_start(bo_sb[:, :], bo[:, :]).then_inc(small_in, DMA)
            for rows, params in zip(bn_rows, (bn1, bn2)):
                for i, p in enumerate(params):
                    sp.dma_start(rows[i * E * KB:(i + 1) * E * KB, :],
                                 p.rearrange("e (k p) -> (e k) p", p=P)).then_inc(small_in, DMA)

            def load_weights(k, i):
                layer, e = task_at(k, i)
                sp.dma_start(w_stage[i % 2][:, :].rearrange("p (k d) -> p k d", k=KB),
                             (W1, W2)[layer][e].rearrange("(k p) d -> p k d", p=P)).then_inc(stage_in[i % 2], DMA)

            def slot(k, u, last):
                ok, t, n = tile_at(k, u, 1, last)
                if ok:
                    wait(sp, S["x1_ready"], n)
                    it = t % TB
                    sp.dma_start(x1_dram[it // CT, 2 * k + t // TB, :, it % CT, :],
                                 x1_sb[t % 4][:, :]).then_inc(x1_stored[t % 4], DMA)
                    if not last and it % 2 == 1:
                        load_x(2 * k + t // TB + 2, t // TB, it // 2)
                ok, t, n = tile_at(k, u, 8, last)
                if ok:
                    wait(sp, S["masked_ready"], n - 2)
                    load_adj(2 * k + t // TB, t % TB, t % 2)
                if u >= 0 and u % TASK_SLOTS == TASK_SLOTS // 2:
                    i = u // TASK_SLOTS + 1
                    if i < TASKS or not last:
                        wait(sp, S["w12_lo_ready"], k * TASKS + (i - 1))
                        load_weights(k + i // TASKS, i % TASKS)
                if last and u == NORM_SLOT - 1:
                    for t in range(CT):
                        sp.wait_ge(x1_stored[t], DMA * 2)
                    sp.dma_start(ffn_x1[:, :, :], x1_dram[0, 0]).then_inc(ffn_x1_in, DMA)

            load_weights(0, 0)
            for u in range(-6, 0):
                slot(0, u, PAIRS == 1)
            if PAIRS > 1:
                with sp.Fori(0, PAIRS - 1) as k:
                    for u in range(UT):
                        slot(k, u, False)
            for u in range(UT):
                slot(PAIRS - 1, u, True)
            for i in range(4):
                sp.wait_ge(x1_stored[i], DMA * (1 + PAIRS * UT // 4))
            sp.wait_ge(small_in, DMA * 13)

        @block.gpsimd
        def _(pool):
            for i in range(4):
                pool.sem_inc(x1_stored[i], DMA)
            pool.sem_inc(S["n1_ready"], 4)
            pool.sem_inc(S["n1_added"], 1)
            pool.memset(ident[:, :], 0.0).then_inc(S["const_zero"], 1)
            pool.memset(minus_half[:, :], -0.5).then_inc(S["const_zero"], 1)
            pool.memset(ln_eps[:, :], LN_EPS).then_inc(S["const_zero"], 1)
            pool.memset(tiny[:, :], TINY).then_inc(S["const_zero"], 1)
            pool.memset(sum_eps[:, :], LN_EPS * D).then_inc(S["const_zero"], 1)
            pool.wait_ge(S["const_zero"], 5)
            pool.affine_select(out=ident[:, :], in_=ident[:, :], compare_op=ALU.not_equal, fill=1.0, base=0,
                               pattern=[[-1, P]], channel_multiplier=1).then_inc(S["const_ready"], 1)
            pool.memset(feat_sum[:, :, :], 0.0).then_inc(S["const_zero"], 1)
            pool.wait_ge(S["const_zero"], 6)

            def head_rstd(c, step):
                i = step % 2
                pool.wait_ge(S["xs_mv_ready"], c)
                pool.tensor_tensor(xs_vareps[:, i, :], xs_mv[:, i, :, 1], ln_eps[:, 0:2], ALU.add) \
                    .then_inc(S["xs_vareps_ready"], 1)
                pool.wait_ge(S["xs_vareps_ready"], c)
                pool.tensor_tensor(xs_rstd[:, i, :], xs_vareps[:, i, :], minus_half[:, 0:2], ALU.pow) \
                    .then_inc(S["xs_rstd_ready"], 1)

            def split_weights_lo(k, i):
                layer, e = task_at(k, i)
                pool.wait_ge(S["w12_hi_ready"], k * TASKS + (i + 1))
                pool.tensor_tensor(w12_lo[:, layer, e, :], w_stage[i % 2][:, :], bits(w12_hi[:, layer, e, :]),
                                   ALU.subtract).then_inc(S["w12_lo_ready"], 1)

            def slot(k, u, last):
                ok, t, n = tile_at(k, u, 2, last)
                if ok:
                    pool.wait_ge(S["probs_ready"], n)
                    pool.tensor_tensor(row_den[:, t % 4:t % 4 + 1], row_sum[:, t % 4:t % 4 + 1], tiny[:, :], ALU.add) \
                        .then_inc(S["den_ready"], 1)
                ok, t, n = tile_at(k, u, 1, last)
                if ok:
                    pool.wait_ge(S["x1_squares_ready"], n)
                    pool.tensor_tensor(x1_vareps[:, t % 4:t % 4 + 1], x1_squares[:, t % 4:t % 4 + 1], sum_eps[:, :],
                                       ALU.add) \
                        .then_inc(S["x1_vareps_ready"], 1)
                    pool.wait_ge(S["x1_vareps_ready"], n)
                    pool.tensor_tensor(x1_rstd[:, t % 4:t % 4 + 1], x1_vareps[:, t % 4:t % 4 + 1],
                                       minus_half[:, 0:1], ALU.pow).then_inc(S["x1_rstd_ready"], 1)
                ok0, t0, n0 = tile_at(k, u, 0, last)
                ok0 = ok0 and t0 >= 0
                ok1, t1, n1 = tile_at(k, u, 1, last)
                if ok0:
                    pool.wait_ge(S["n1_ready"], n0 + 4)
                    if ok1:
                        pool.wait_ge(S["x1_rstd_ready"], n1)
                    pool.wait_ge(S["n1_added"], n0)
                    rows = feat_sum[:, t0 % TB, :]
                    pool.tensor_tensor(rows, rows, n1_sb[t0 % 2][:, :], ALU.add).then_inc(S["n1_added"], 1)
                if ok1:
                    if not ok0:
                        pool.wait_ge(S["x1_rstd_ready"], n1)
                    pool.tensor_scalar(n1_sb[t1 % 2][:, :], x1_sb[t1 % 4][:, :], x1_mean[:, t1 % 4:t1 % 4 + 1],
                                       x1_rstd[:, t1 % 4:t1 % 4 + 1], ALU.subtract, ALU.mult) \
                        .then_inc(S["n1_ready"], 1)
                head = head_at(k, u, last)
                if head and head[1] < HEADS:
                    head_rstd((2 * k + head[0]) * HEADS + (head[1] + 1), head[1])
                if u >= 0 and u % TASK_SLOTS == TASK_SLOTS // 2:
                    split_weights_lo(k, u // TASK_SLOTS)
                if last and u == NORM_SLOT + 1:
                    norm.deviation(pool, 1)

            for j in range(HEADS):
                head_rstd(j + 1, j)
            pool.wait_ge(S["bn_eps_ready"], 1)
            pool.tensor_tensor(bn_rsqrt[:, :, :].rearrange("p i c -> p (i c)"),
                               bn_eps[:, :, :].rearrange("p i c -> p (i c)"),
                               minus_half[:, 0:1].to_broadcast([P, 2 * EK]), ALU.pow).then_inc(S["bn_rsqrt_ready"], 1)
            for u in range(-6, 0):
                slot(0, u, PAIRS == 1)
            if PAIRS > 1:
                with pool.Fori(0, PAIRS - 1) as k:
                    for u in range(UT):
                        slot(k, u, False)
            for u in range(UT):
                slot(PAIRS - 1, u, True)

        @block.tensor
        def _(pe):
            pe.wait_ge(S["const_ready"], 1)
            pe.wait_ge(S["w_centred_ready"], 1)
            pe.wait_ge(S["a_scaled"], 1)
            for d in range(KB):
                for o in range(KB):
                    pe.transpose(head_ps[:, d, o * P:(o + 1) * P], w_centred[:, o, d * P:(d + 1) * P], ident[:, :])
                for o in range(KB):
                    last = pe.matmul(head_ps[:, d, D:DX], w_centred[:, o, d * P:(d + 1) * P], a_sb[:, o, :],
                                     start=(o == 0), stop=(o == KB - 1))
            last.then_inc(S["wT_ready"], 1)

            def head_transpose(b, j, i, turn, first=False):
                xT, _, _ = (first_head if first else later_head)(j)
                if j == 0:
                    wait(pe, S["ej_rows_ready"], b)
                elif not first:
                    pe.wait_ge(S["wh_lo_ready"], b * TB + 2 * j)
                pe.wait_ge(x_in[i][j], DMA * turn)
                for c in range(2):
                    for d in range(KB):
                        at = d * 2 * P + c * P
                        last = pe.transpose(xT[:, at:at + P], x_sb[i][:, 2 * j + c, d * P:(d + 1) * P],
                                            ident[:, :])
                last.then_inc(S["hT_psum"], 1)

            def head_project(b, j, first=False):
                _, hT_j, acc = (first_head if first else later_head)(j)
                if first and j >= 2:
                    pe.wait_ge(S["wh_lo_ready"], 2 * (j - 1))
                pe.wait_ge(S["hT_ready"], b * HEADS + (j + 1))
                for c in range(2):
                    for d in range(KB):
                        cols = slice(c * P, (c + 1) * P)
                        last = pe.matmul(acc[:, 1 - c, 0:DX], hT_j[:, d, cols], wx[:, d, :],
                                         start=(d == 0), stop=(d == KB - 1))
                    last.then_inc(S["wh_ready"], 1)

            def spread_ej(b, i):
                pe.wait_ge(S["wh_lo_ready"], b * TB + TB)
                for t in range(TB):
                    at = (t % CT) * P
                    last = pe.transpose(head_ps[:, t // CT, at:at + P],
                                        e_cols[i][:, t ^ 1, 1:2].to_broadcast([P, P]), ident[:, :])
                    if t % CT == CT - 1:
                        last.then_inc(S["ej_rows_psum"], 1)

            def slot(k, u, last_pair):
                head = head_at(k, u, last_pair)
                if head and head[1] == HEADS + 1:
                    spread_ej(2 * k + head[0], head[0] % 2)
                ok, t, n = tile_at(k, u, 3, last_pair)
                if ok:
                    pe.wait_ge(S["probs_ready"], n)
                    wait(pe, S["pT_lo_ready"], n - 2)
                    for j in range(TB):
                        last = pe.transpose(pT_ps[t % 2][:, j, :], scores[t % 4][:, j * P:(j + 1) * P], ident[:, :])
                    last.then_inc(S["pT_ready"], 1)
                if head and 1 <= head[1] <= HEADS:
                    head_project(2 * k + head[0], head[1] - 1)
                ok, t, n = tile_at(k, u, 2, last_pair)
                if ok:
                    pe.wait_ge(S["pT_lo_ready"], n)
                    wait(pe, S["x1_ready"], n - 2)
                    i, acc = parity(t), attn_ps[:, t % 2, 0:D]
                    for j in range(TB):
                        last = split_matmul(pe, acc, pT_hi[t % 2][:, j, :], pT_lo[t % 2][:, j, :],
                                            wh_hi[i][:, j, :], wh_lo[i][:, j, :], j == 0, j == TB - 1)
                    last.then_inc(S["attn_ready"], 1)
                if head and head[1] < HEADS:
                    head_transpose(2 * k + head[0], head[1], head[0] % 2, k + (head[0] // 2 + 1))

            head_transpose(0, 0, 0, 1, first=True)
            head_transpose(0, 1, 0, 1, first=True)
            pe.wait_ge(S["wx_ready"], 1)
            for j in range(HEADS):
                head_project(0, j, first=True)
                if j + 2 < HEADS:
                    head_transpose(0, j + 2, 0, 1, first=True)
            spread_ej(0, 0)
            pe.wait_ge(small_in, 13 * DMA)
            for i in range(2):
                last = pe.transpose(attn_ps[:, i, 0:5 * EK], bn_rows[i][:, :], ident[0:5 * EK, 0:5 * EK])
            last.then_inc(S["bn_psum"], 1)
            for u in range(-6, 0):
                slot(0, u, PAIRS == 1)
            if PAIRS > 1:
                with pe.Fori(0, PAIRS - 1) as k:
                    for u in range(UT):
                        slot(k, u, False)
            for u in range(UT):
                slot(PAIRS - 1, u, True)

        @block.scalar
        def _(act):
            act.wait_ge(S["wT_ready"], 1)
            act.activation(wx[:, :, :], head_ps[:, :, 0:DX], ACT.Copy).then_inc(S["wx_ready"], 1)

            def head_hT(b, j, first=False):
                xT, hT_j, _ = (first_head if first else later_head)(j)
                act.wait_ge(S["hT_psum"], b * HEADS + (j + 1))
                act.activation(hT_j.rearrange("p k c -> p (k c)"), xT, ACT.Copy) \
                    .then_inc(S["hT_ready"], 1)

            def head_wh(b, j, i, first=False):
                _, _, acc = (first_head if first else later_head)(j)
                act.wait_ge(S["xs_rstd_ready"], b * HEADS + (j + 1))
                for c in range(2):
                    t = 2 * j + c
                    act.wait_ge(S["wh_ready"], b * TB + (t + 1))
                    act.activation(wh_hi[i][:, t, :], acc[:, 1 - c, 0:D], ACT.Copy,
                                   scale=xs_rstd[:, j % 2, 1 - c:2 - c]).then_inc(S["wh_hi_ready"], 1)

            def head_ej(b, i):
                for h in range(2):
                    act.wait_ge(S["ej_rows_psum"], 2 * b + (h + 1))
                    last = act.activation(ej_rows[i][:, h * BANK:(h + 1) * BANK], head_ps[:, h, :], ACT.Copy,
                                          scale=-EDGE_UNIT)
                last.then_inc(S["ej_rows_ready"], 1)

            def split_weights_hi(k, i):
                layer, e = task_at(k, i)
                act.wait_ge(stage_in[i % 2], DMA * (k * EP + (i // 2 + 1)))
                act.activation(w12_hi[:, layer, e, :], w_stage[i % 2][:, :], ACT.Copy).then_inc(S["w12_hi_ready"], 1)

            def relu(k, u, last):
                ok, t, n = tile_at(k, u, 5, last)
                if ok:
                    act.wait_ge(S["masked_ready"], n)
                    wait(act, S["lrelu_ready"], n - 2)
                    act.activation(upper[t % 2][:, :], scores[t % 4][:, :], ACT.Relu, scale=1.0 - 1.0 / SLOPE,
                                   bias=e_cols[parity(t)][:, (t % TB) ^ 1, 0:1]).then_inc(S["upper_ready"], 1)

            def upper_half(k, u, last):
                ok, t, n = tile_at(k, u, 3, last)
                if ok:
                    act.wait_ge(S["pT_ready"], n)
                    wait(act, S["attn_ready"], n - 2)
                    act.activation(pT_hi[t % 2][:, :, :], pT_ps[t % 2][:, :, :], ACT.Copy) \
                        .then_inc(S["pT_hi_ready"], 1)

            def slot(k, u, last):
                head = head_at(k, u, last)
                if head and 1 <= head[1] <= HEADS:
                    head_hT(2 * k + head[0], head[1] - 1)
                if head and head[1] == HEADS + 1:
                    head_ej(2 * k + head[0], head[0] % 2)
                if head and 1 <= head[1] <= HEADS:
                    upper_half(k, u, last)
                    relu(k, u, last)
                else:
                    relu(k, u, last)
                    upper_half(k, u, last)
                if head and 1 <= head[1] <= HEADS:
                    head_wh(2 * k + head[0], head[1] - 1, head[0] % 2)
                post, pt, pn = tile_at(k, u, 1, last)
                ok, t, n = tile_at(k, u, 4, last)
                c, pc = slice(t % 4, t % 4 + 1), slice(pt % 4, pt % 4 + 1)
                if post:
                    act.wait_ge(S["x1_ready"], pn)
                    act.activation(x1_mean[:, pc], x1_sum[:, pc], ACT.Copy, scale=1.0 / D) \
                        .then_inc(S["x1_mean_ready"], 1)
                if ok:
                    act.wait_ge(S["lrelu_ready"], n)
                    act.activation(neg_max[:, c], row_max[:, c], ACT.Copy, scale=-1.0).then_inc(S["negmax_ready"], 1)
                if post:
                    act.wait_ge(S["x1_mean_ready"], pn)
                    act.activation(x1_deviation, x1_sb[pt % 4][:, :], ACT.Square, scale=-1.0, bias=x1_mean[:, pc],
                                   accum_out=x1_squares[:, pc]).then_inc(S["x1_squares_ready"], 1)
                if ok:
                    act.wait_ge(S["negmax_ready"], n)
                    act.activation(scores[t % 4][:, :], scores[t % 4][:, :], ACT.Exp, bias=neg_max[:, c],
                                   accum_out=row_sum[:, c]).then_inc(S["probs_ready"], 1)
                if u >= 0 and u % TASK_SLOTS == TASK_SLOTS // 2:
                    split_weights_hi(k, u // TASK_SLOTS)

            head_hT(0, 0, first=True)
            head_hT(0, 1, first=True)
            for j in range(HEADS):
                head_wh(0, j, 0, first=True)
                if j + 2 < HEADS:
                    head_hT(0, j + 2, first=True)
            head_ej(0, 0)
            for u in range(-6, 0):
                slot(0, u, PAIRS == 1)
            if PAIRS > 1:
                with act.Fori(0, PAIRS - 1) as k:
                    for u in range(UT):
                        slot(k, u, False)
            for u in range(UT):
                slot(PAIRS - 1, u, True)

        @block.vector
        def _(dve):
            dve.wait_ge(w_in, 3 * DMA)
            for o in range(KB):
                dve.bn_stats(w_stats[:, o, :], w_sb[:, o, :]).then_inc(S["w_stat"], 1)
            dve.wait_ge(S["w_stat"], KB)
            for o in range(KB):
                dve.bn_aggr(w_mv[:, o, :], w_stats[:, o, :]).then_inc(S["w_mv_ready"], 1)
            dve.wait_ge(S["w_mv_ready"], KB)
            for o in range(KB):
                last = dve.tensor_scalar(w_centred[:, o, :], w_sb[:, o, :], w_mv[:, o, 0:1], None, ALU.subtract)
            last.then_inc(S["w_centred_ready"], 1)
            dve.tensor_scalar(a_sb[:, :, 0], a_sb[:, :, 0], (1.0 / SLOPE - 1.0) * EDGE_UNIT, None, ALU.mult) \
                .then_inc(S["a_scaled"], 1)

            def head_stats(b, j, i, turn):
                dve.wait_ge(x_in[i][j], DMA * turn)
                for c in range(2):
                    dve.bn_stats(xs_stats[:, j % 2, c, :], x_sb[i][:, 2 * j + c, :]).then_inc(S["xs_stat"], 1)

            def head_mean_var(b, j, waited):
                if not waited:
                    dve.wait_ge(S["xs_stat"], 2 * (b * HEADS + (j + 1)))
                for c in range(2):
                    last = dve.bn_aggr(xs_mv[:, j % 2, 1 - c, :], xs_stats[:, j % 2, c, :])
                last.then_inc(S["xs_mv_ready"], 1)

            def head_wh(b, j, i, first=False):
                _, _, acc = (first_head if first else later_head)(j)
                for c in range(2):
                    t, rstd = 2 * j + c, xs_rstd[:, j % 2, 1 - c:2 - c]
                    dve.wait_ge(S["wh_hi_ready"], b * TB + (t + 1))
                    if c == 1:
                        dve.tensor_tensor(e_cols[i][:, t - 1:t + 1, :], acc[:, :, D:DX],
                                          xs_rstd[:, j % 2, :].unsqueeze(2).to_broadcast([P, 2, 2]), ALU.mult)
                    dve.scalar_tensor_tensor(wh_lo[i][:, t, :], acc[:, 1 - c, 0:D], rstd, bits(wh_hi[i][:, t, :]),
                                             ALU.mult, ALU.subtract).then_inc(S["wh_lo_ready"], 1)

            def slot(k, u, last):
                head = head_at(k, u, last)
                step = head[1] if head else None
                hb, hi = (2 * k + head[0], head[0] % 2) if head else (None, None)
                post, pt, pn = tile_at(k, u, 1, last)
                pc = pt % 4
                ok, t, n = tile_at(k, u, 4, last)
                if ok:
                    c = t % 4
                    if post:
                        dve.wait_ge(S["upper_ready"], n)
                        invert_sum(pc, pn)
                    else:
                        dve.wait_ge(S["upper_ready"], n)
                    dve.tensor_tensor_reduce(out=scores[c][:, :], in0=upper[t % 2][:, :], in1=scores[c][:, :],
                                             scale=SLOPE / EDGE_UNIT, scalar=-0.5 * SLOPE / EDGE_UNIT,
                                             op0=ALU.subtract, op1=ALU.max, accum_out=row_max[:, c:c + 1]) \
                        .then_inc(S["lrelu_ready"], 1)
                else:
                    if post:
                        invert_sum(pc, pn)
                if post:
                    dve.wait_ge(S["inv_ready"], pn)
                    dve.wait_ge(S["attn_ready"], pn)
                    dve.wait_ge(x1_stored[pc], DMA * (k * (UT // 4) + (pt // 4 + 1)))
                    dve.wait_ge(S["n1_ready"], pn)
                    dve.scalar_tensor_tensor(x1_sb[pc][:, :], attn_ps[:, pt % 2, 0:D], row_inv[:, pc:pc + 1],
                                             x_sb[parity(pt)][:, pt % TB, :], ALU.mult, ALU.add,
                                             accum_out=x1_sum[:, pc:pc + 1]).then_inc(S["x1_ready"], 1)
                stats = bool(head) and step < HEADS
                if stats:
                    head_stats(hb, step, hi, k + (head[0] // 2 + 1))
                ok, t, n = tile_at(k, u, 6, last)
                if ok:
                    dve.wait_ge(adj_in[t % 2], DMA * (k * (UT // 2) + (t // 2 + 1)))
                    if t % TB == 0:
                        dve.wait_ge(S["ej_rows_ready"], 2 * k + (t // TB + 1))
                    wait(dve, S["pT_ready"], n - 4)
                    dve.scalar_tensor_tensor(scores[t % 4][:, :], adj_sb[t % 2][:, :], 0.0, ej_rows[parity(t)][:, :],
                                             ALU.is_equal, ALU.add).then_inc(S["masked_ready"], 1)
                ok, t, n = tile_at(k, u, 3, last)
                if ok:
                    if stats:
                        dve.wait_ge(S["xs_stat"], 2 * (hb * HEADS + step + 1))
                    dve.wait_ge(S["pT_hi_ready"], n)
                    wait(dve, S["attn_ready"], n - 2)
                    dve.tensor_tensor(pT_lo[t % 2][:, :, :], pT_ps[t % 2][:, :, :], bits(pT_hi[t % 2][:, :, :]),
                                      ALU.subtract).then_inc(S["pT_lo_ready"], 1)
                if stats:
                    head_mean_var(hb, step, ok)
                if head and 1 <= step <= HEADS:
                    head_wh(hb, step - 1, hi)
                if last and u == NORM_SLOT:
                    norm.statistics(dve, ffn_x1, ffn_x1_in, 1)
                if last and u == NORM_SLOT + 1:
                    norm.mean_var(dve, 1, False)
                if last and u == NORM_SLOT + 2:
                    norm.normalise(dve, ffn_x1, 1)

            def invert_sum(c, n):
                dve.wait_ge(S["den_ready"], n)
                dve.reciprocal(row_inv[:, c:c + 1], row_den[:, c:c + 1]).then_inc(S["inv_ready"], 1)

            for j in range(HEADS + 1):
                if j < HEADS:
                    head_stats(0, j, 0, 1)
                    head_mean_var(0, j, False)
                if j > 0:
                    head_wh(0, j - 1, 0, first=True)
            def batch_norms():
                dve.wait_ge(S["bn_rsqrt_ready"], 1)
                for i in range(2):
                    dve.tensor_tensor(bn_scale[i][:, :], bn_rsqrt[:, i, :], bn_cols[i][:, GAMMA, :], ALU.mult) \
                        .then_inc(S["bn_scale_ready"], 1)
                    dve.tensor_tensor(bn_diff[:, i, :], bn_cols[i][:, BIAS, :], bn_cols[i][:, MEAN, :], ALU.subtract) \
                        .then_inc(S["bn_diff_ready"], 1)
                for i in range(2):
                    dve.wait_ge(S["bn_scale_ready"], i + 1)
                    dve.wait_ge(S["bn_diff_ready"], i + 1)
                    dve.tensor_tensor(bn_eps[:, i, :], bn_diff[:, i, :], bn_scale[i][:, :], ALU.mult) \
                        .then_inc(S["bn_prod_ready"], 1)
                for i in range(2):
                    dve.wait_ge(S["bn_prod_ready"], i + 1)
                    dve.tensor_tensor(bn_shift[i][:, :], bn_eps[:, i, :], bn_cols[i][:, BETA, :], ALU.add)

            BIAS, GAMMA, BETA, MEAN, VAR = range(5)
            dve.wait_ge(S["bn_psum"], 1)
            for i in range(2):
                last = dve.tensor_copy(bn_cols[i][:, :, :].rearrange("p i c -> p (i c)"), attn_ps[:, i, 0:5 * EK])
            last.then_inc(S["bn_cols_ready"], 1)
            dve.wait_ge(S["bn_cols_ready"], 1)
            for i in range(2):
                last = dve.tensor_scalar(bn_eps[:, i, :], bn_cols[i][:, VAR, :], BN_EPS, None, ALU.add)
            last.then_inc(S["bn_eps_ready"], 1)
            for u in range(-6, 0):
                slot(0, u, PAIRS == 1)
                if u == -4:
                    batch_norms()
            if PAIRS > 1:
                with dve.Fori(0, PAIRS - 1) as k:
                    for u in range(UT):
                        slot(k, u, False)
            for u in range(UT):
                slot(PAIRS - 1, u, True)


def ffn_block(nc, B, Wo, x1_dram, w_dram, out, ident, minus_half, node_table, w12_hi, w12_lo,
              wr_sb, br_sb, bo_sb, bn_scale, bn_shift, norm, x1_first, x1_first_in):
    TB, D = node_table.shape[1], node_table.shape[2]
    E, KB = wr_sb.shape[2], D // P
    CT, CH = BANK // P, TB * P // BANK
    WP = E // 4
    WL = WP * KB * D
    US = CH * E
    LOOK = 3

    ctx = ExitStack()
    with ctx:
        def sb(name, shape, dt=FP32):
            return ctx.enter_context(nc.sbuf_tensor(name, shape, dt))

        def ps(name):
            return ctx.enter_context(nc.psum_tensor(name, [P, KB, BANK], FP32))

        def sem(name):
            return ctx.enter_context(nc.semaphore(name))

        w_bc = sb("w_bc", [P, CH, E, BANK])
        wo_hi, wo_lo = sb("wo_hi", [P, E, KB * D], FP32R), sb("wo_lo", [P, E, KB * D], FP32R)
        logits, expd, w_sb = (sb(f"gate_{n}", [P, TB, E]) for n in ("logits", "expd", "w"))
        top, total, inv = (sb(f"gate_{n}", [P, TB]) for n in ("top", "total", "inv"))

        x1_sb = [x1_first, sb("ffn_x11", [P, CT, D])]
        xT_hi, xT_lo = sb("xT_hi", [P, KB, BANK], FP32R), sb("xT_lo", [P, KB, BANK], FP32R)
        h1 = sb("h1", [P, KB, BANK])
        h1_hi = [sb(f"h1_hi{i}", [P, KB, BANK], FP32R) for i in range(2)]
        h1_lo = [sb(f"h1_lo{i}", [P, KB, BANK], FP32R) for i in range(2)]
        h2 = sb("h2", [P, KB, BANK])
        h2_hi = [sb(f"h2_hi{i}", [P, KB, BANK], FP32R) for i in range(2)]
        h2_lo = [sb(f"h2_lo{i}", [P, KB, BANK], FP32R) for i in range(2)]
        yT_sb = sb("yT_sb", [P, KB, BANK])
        wT_sb = yT_sb[0:E, :, :].rearrange("e c n -> e (c n)")
        wo_stage = w_bc[:, :, :, :].rearrange("p a b c -> p (a b c)")
        featT = w_bo = node_table

        z1_ps, z2_ps, y_ps, turn_ps = ps("z1_ps"), ps("z2_ps"), ps("y_ps"), ps("turn_ps")

        x1_in = [x1_first_in, sem("ffn_x1_in1")]
        stored = [sem(f"ffn_stored{i}") for i in range(2)]
        wo_in = [sem(f"wo_in{i}") for i in range(4)]
        w_stored, w_bc_in = sem("w_stored"), [sem(f"w_bc_in{e}") for e in range(E)]
        names = """residual_ready xT_psum xT_hi_ready xT_lo_ready
            z1_ready h1_ready h1_hi_ready h1_lo_ready z2_ready relu2_ready gated_ready h2_hi_ready h2_lo_ready
            step_done yT_ready out_psum out_ready
            featT_psum featT_ready logits_psum logits_ready top_ready centred_ready exp_ready total_ready
            inv_ready w_ready wT_psum wT_ready table_psum table_ready
            wo_hi_ready wo_lo_ready wo_lo_pool_ready""".split()
        S = {n: sem(f"ffn_{n}") for n in names}

        def step_at(b, u, off, last):
            t = u + off
            ok = t >= 0 and (t < US or not last)
            return ok, (t // E) % CH, t % E, b * US + (t + 1)

        def next_tile(b, u, last):
            t = u // E + 1
            return t >= 1 and (t < CH or not last), t % CH, b * CH + (t + 1)

        block = ctx.enter_context(nc.Block())

        @block.sync
        def _(sp):
            def load(b, c):
                sp.dma_start(x1_sb[c][:, :, :], x1_dram[c, b]).then_inc(x1_in[c], DMA)

            def store(b, c, last):
                wait(sp, S["out_ready"], b * CH + (c + 1))
                sp.dma_start(out[b].rearrange("(c s p) d -> c p s d", c=CH, p=P)[c], x1_sb[c][:, :, :]) \
                    .then_inc(stored[c], DMA)
                if not last:
                    sp.wait_ge(stored[c], DMA * (b + 1))
                    load(b + 1, c)

            for i in range(4):
                sp.dma_start(wo_stage[:, i * WL:(i + 1) * WL].rearrange("p (e k d) -> p e k d", e=WP, k=KB),
                             Wo[i * WP:(i + 1) * WP].rearrange("e (k p) d -> p e k d", p=P)).then_inc(wo_in[i], DMA)
            load(0, 1)
            sp.wait_ge(S["wT_ready"], 1)
            sp.dma_start(w_dram.rearrange("e c n -> e (c n)"), wT_sb).then_inc(w_stored, DMA)
            sp.wait_ge(w_stored, DMA)
            sp.wait_ge(S["wo_lo_ready"], 2)
            sp.wait_ge(S["wo_lo_pool_ready"], 2)
            for e in range(E):
                sp.dma_start(w_bc[:, :, e, :], w_dram[e].partition_broadcast(P)).then_inc(w_bc_in[e], DMA)
            if B > 1:
                with sp.Fori(0, B - 1) as b:
                    for c in range(CH):
                        store(b, c, False)
            for c in range(CH):
                store(B - 1, c, True)
            for c in range(CH):
                sp.wait_ge(stored[c], DMA * B)

        @block.gpsimd
        def _(pool):
            def residual(c, n):
                pool.wait_ge(norm.xn_ready, n)
                pool.tensor_tensor(x1_sb[c][:, :, :], x1_sb[c][:, :, :], w_bo[:, c * CT:(c + 1) * CT, :], ALU.add) \
                    .then_inc(S["residual_ready"], 1)

            for i in (2, 3):
                part = slice(i * WP, (i + 1) * WP)
                pool.wait_ge(S["wo_hi_ready"], i + 1)
                pool.tensor_tensor(wo_lo[:, part, :].rearrange("p e c -> p (e c)"), wo_stage[:, i * WL:(i + 1) * WL],
                                   bits(wo_hi[:, part, :]).rearrange("p e c -> p (e c)"), ALU.subtract) \
                    .then_inc(S["wo_lo_pool_ready"], 1)
            pool.wait_ge(S["table_ready"], 1)
            if B > 1:
                with pool.Fori(0, B - 1) as b:
                    for c in range(CH):
                        residual(c, b * CH + (c + 1))
                        norm.deviation(pool, b * CH + (c + 2))
            for c in range(CH):
                residual(c, (B - 1) * CH + (c + 1))
                if c + 1 < CH:
                    norm.deviation(pool, (B - 1) * CH + (c + 2))

        @block.tensor
        def _(pe):
            def transpose_x(n):
                pe.wait_ge(norm.xn_ready, n)
                wait(pe, S["out_ready"], n - 2)
                for d in range(KB):
                    for s in range(CT):
                        last = pe.transpose(turn_ps[:, d, s * P:(s + 1) * P], norm.xn[:, s, d * P:(d + 1) * P],
                                            ident[:, :])
                last.then_inc(S["xT_psum"], 1)

            def transpose_y(n):
                pe.wait_ge(S["yT_ready"], n)
                for s in range(CT):
                    for d in range(KB):
                        at = (s % 2) * D + d * P
                        last = pe.transpose(turn_ps[:, s // 2, at:at + P], yT_sb[:, d, s * P:(s + 1) * P], ident[:, :])
                last.then_inc(S["out_psum"], 1)

            def layer(acc, w_hi, w_lo, x_hi, x_lo, first, last):
                for m in range(KB):
                    for k in range(KB):
                        at = slice(k * D + m * P, k * D + (m + 1) * P)
                        done = split_matmul(pe, acc[:, m, :], w_hi[:, at], w_lo[:, at], x_hi[:, k, :], x_lo[:, k, :],
                                            first and k == 0, last and k == KB - 1)
                return done

            def transpose_gate():
                pe.wait_ge(S["w_ready"], 1)
                for it in range(TB):
                    last = pe.transpose(y_ps[0:E, it // CT, (it % CT) * P:(it % CT + 1) * P], w_sb[:, it, :],
                                        ident[:, :])
                last.then_inc(S["wT_psum"], 1)

            def gate_bias():
                pe.wait_ge(S["wT_ready"], 1)
                for it in range(TB):
                    acc = (y_ps, turn_ps)[it // CT]
                    last = pe.matmul(acc[:, (it % CT) // 2, (it % 2) * D:(it % 2 + 1) * D],
                                     wT_sb[:, it * P:(it + 1) * P], bo_sb[:, :], start=True, stop=True)
                last.then_inc(S["table_psum"], 1)

            def slot(b, u, last):
                ok, c, e, n = step_at(b, u, 3, last)
                if ok:
                    if e == 0:
                        pe.wait_ge(S["xT_lo_ready"], b * CH + ((u + 3) // E + 1))
                    wait(pe, S["h1_ready"], n - 1)
                    layer(z1_ps, w12_hi[:, 0, e, :], w12_lo[:, 0, e, :], xT_hi, xT_lo, True, True) \
                        .then_inc(S["z1_ready"], 1)
                if u == -2:
                    transpose_gate()
                if u == -1:
                    gate_bias()
                ok, _, n = next_tile(b, u, last)
                if ok and u % E == 4:
                    transpose_x(n)
                if u >= 0 and u % E == E - 1:
                    transpose_y(b * CH + (u // E + 1))
                ok, c, e, n = step_at(b, u, 2, last)
                if ok:
                    pe.wait_ge(S["h1_lo_ready"], n)
                    wait(pe, S["relu2_ready"], n - 1)
                    layer(z2_ps, w12_hi[:, 1, e, :], w12_lo[:, 1, e, :], h1_hi[n_par(u + 2)], h1_lo[n_par(u + 2)],
                          True, True).then_inc(S["z2_ready"], 1)
                ok, c, e, n = step_at(b, u, 1, last)
                if ok:
                    pe.wait_ge(S["h2_lo_ready"], n)
                    if u == -1:
                        pe.wait_ge(S["table_ready"], 1)
                        pe.wait_ge(S["wo_lo_ready"], 2)
                        pe.wait_ge(S["wo_lo_pool_ready"], 2)
                    if e == 0:
                        wait(pe, S["yT_ready"], b * CH + (u + 1) // E)
                    layer(y_ps, wo_hi[:, e, :], wo_lo[:, e, :], h2_hi[n_par(u + 1)], h2_lo[n_par(u + 1)],
                          e == 0, e == E - 1).then_inc(S["step_done"], 1)

            transpose_x(1)
            for it in range(TB):
                for d in range(KB):
                    acc, at = (z2_ps, y_ps)[it // CT], ((it % CT) * KB + d) * P
                    last = pe.transpose(acc[:, at // BANK, at % BANK:at % BANK + P],
                                        node_table[:, it, d * P:(d + 1) * P], ident[:, :])
            last.then_inc(S["featT_psum"], 1)
            slot(0, -3, B == 1)
            pe.wait_ge(S["featT_ready"], 1)
            for it in range(TB):
                for d in range(KB):
                    last = pe.matmul(y_ps[:, 0, it * E:(it + 1) * E], featT[:, it, d * P:(d + 1) * P], wr_sb[:, d, :],
                                     start=(d == 0), stop=(d == KB - 1))
            last.then_inc(S["logits_psum"], 1)
            for u in range(1 - LOOK, 0):
                slot(0, u, B == 1)
            if B > 1:
                with pe.Fori(0, B - 1) as b:
                    for u in range(US):
                        slot(b, u, False)
            for u in range(US):
                slot(B - 1, u, True)

        @block.scalar
        def _(act):
            def split_x(n):
                act.wait_ge(S["xT_psum"], n)
                act.activation(xT_hi[:, :, :], turn_ps[:, :, :], ACT.Copy).then_inc(S["xT_hi_ready"], 1)

            def copy_gate():
                act.wait_ge(S["wT_psum"], 1)
                act.activation(wT_sb, y_ps[0:E, :, :].rearrange("e k c -> e (k c)"), ACT.Copy) \
                    .then_inc(S["wT_ready"], 1)

            def copy_gate_bias():
                act.wait_ge(S["table_psum"], 1)
                for i, acc in enumerate((y_ps, turn_ps)):
                    last = act.activation(w_bo[:, i * CT:(i + 1) * CT, :].rearrange("p t d -> p (t d)"),
                                          acc[:, :, :].rearrange("p k c -> p (k c)"), ACT.Copy)
                last.then_inc(S["table_ready"], 1)

            def bn_relu(dst, src, layer, e, m):
                col = slice(e * KB + m, e * KB + m + 1)
                return act.activation(dst[:, m, :], src[:, m, :], ACT.Relu, bias=bn_shift[layer][:, col],
                                      scale=bn_scale[layer][:, col])

            def slot(b, u, last):
                if u >= 0 and u % E == E - 1:
                    act.wait_ge(S["step_done"], b * US + (u + 1))
                    act.activation(yT_sb[:, :, :], y_ps[:, :, :], ACT.Copy).then_inc(S["yT_ready"], 1)
                ok, c, e, n = step_at(b, u, 3, last)
                if ok:
                    act.wait_ge(S["z1_ready"], n)
                    wait(act, S["h1_lo_ready"], n - 1)
                    for m in range(KB):
                        done = bn_relu(h1, z1_ps, 0, e, m)
                    done.then_inc(S["h1_ready"], 1)
                    act.wait_ge(S["h1_ready"], n)
                    wait(act, S["z2_ready"], n - 2)
                    act.activation(h1_hi[n_par(u + 3)][:, :, :], h1[:, :, :], ACT.Copy).then_inc(S["h1_hi_ready"], 1)
                if u == -2:
                    copy_gate()
                if u == -1:
                    copy_gate_bias()
                ok, _, n = next_tile(b, u, last)
                if ok and u % E == 4:
                    act.wait_ge(S["z1_ready"], b * US + (u + 3 + 1))
                    split_x(n)
                ok, c, e, n = step_at(b, u, 2, last)
                if ok:
                    act.wait_ge(S["z2_ready"], n)
                    wait(act, S["h2_lo_ready"], n - 1)
                    for m in range(KB):
                        done = bn_relu(h2, z2_ps, 1, e, m)
                    done.then_inc(S["relu2_ready"], 1)

            def wo_upper(i):
                part = slice(i * WP, (i + 1) * WP)
                act.wait_ge(wo_in[i], DMA)
                act.activation(wo_hi[:, part, :].rearrange("p e c -> p (e c)"), wo_stage[:, i * WL:(i + 1) * WL],
                               ACT.Copy) \
                    .then_inc(S["wo_hi_ready"], 1)

            split_x(1)
            act.wait_ge(S["featT_psum"], 1)
            for i, acc in enumerate((z2_ps, y_ps)):
                last = act.activation(featT[:, i * CT:(i + 1) * CT, :].rearrange("p t d -> p (t d)"),
                                      acc[:, :, :].rearrange("p k c -> p (k c)"), ACT.Copy, scale=float(D) ** 0.5 / B)
            last.then_inc(S["featT_ready"], 1)
            slot(0, -3, B == 1)
            for i in range(2):
                wo_upper(i)
            act.wait_ge(S["centred_ready"], 1)
            act.activation(expd[:, :, :], logits[:, :, :], ACT.Exp).then_inc(S["exp_ready"], 1)
            for i in range(2, 4):
                wo_upper(i)
            for u in range(1 - LOOK, 0):
                slot(0, u, B == 1)
            if B > 1:
                with act.Fori(0, B - 1) as b:
                    for u in range(US):
                        slot(b, u, False)
            for u in range(US):
                slot(B - 1, u, True)

        @block.vector
        def _(dve):
            def split_x(n):
                dve.wait_ge(S["xT_hi_ready"], n)
                dve.tensor_tensor(xT_lo[:, :, :], turn_ps[:, :, :], bits(xT_hi[:, :, :]), ALU.subtract) \
                    .then_inc(S["xT_lo_ready"], 1)

            def slot(b, u, last):
                tile_ok, tc, tn = next_tile(b, u, last)
                ok, c, e, n = step_at(b, u, 3, last)
                if ok:
                    i = n_par(u + 3)
                    if tile_ok and u % E == 2:
                        dve.wait_ge(norm.stat, CT * tn)
                    dve.wait_ge(S["h1_hi_ready"], n)
                    dve.tensor_tensor(h1_lo[i][:, :, :], h1[:, :, :], bits(h1_hi[i][:, :, :]), ALU.subtract) \
                        .then_inc(S["h1_lo_ready"], 1)
                if tile_ok and u % E == 2:
                    norm.mean_var(dve, tn, ok)
                if tile_ok and u % E == 4:
                    split_x(tn)
                ok, c, e, n = step_at(b, u, 2, last)
                if ok:
                    i = n_par(u + 2)
                    if c == 0:
                        dve.wait_ge(w_bc_in[e], DMA)
                    dve.wait_ge(S["relu2_ready"], n)
                    dve.tensor_tensor(h2[:, :, :], h2[:, :, :], w_bc[:, c, e, :].unsqueeze(1).to_broadcast([P, KB, BANK]),
                                      ALU.mult).then_inc(S["gated_ready"], 1)
                    dve.wait_ge(S["gated_ready"], n)
                    wait(dve, S["step_done"], n - 2)
                    dve.tensor_copy(h2_hi[i][:, :, :], h2[:, :, :]).then_inc(S["h2_hi_ready"], 1)
                    dve.wait_ge(S["h2_hi_ready"], n)
                    dve.tensor_tensor(h2_lo[i][:, :, :], h2[:, :, :], bits(h2_hi[i][:, :, :]), ALU.subtract) \
                        .then_inc(S["h2_lo_ready"], 1)
                if u >= 0 and u % E == E - 1:
                    t = u // E
                    dve.wait_ge(S["out_psum"], b * CH + (t + 1))
                    dve.wait_ge(S["residual_ready"], b * CH + (t + 1))
                    rows = x1_sb[t][:, :, :].rearrange("p s d -> p (s d)")
                    dve.tensor_tensor(rows, turn_ps[:, :, :].rearrange("p k c -> p (k c)"), rows, ALU.add) \
                        .then_inc(S["out_ready"], 1)
                if tile_ok and u % E == 1:
                    norm.statistics(dve, x1_sb[tc], x1_in[tc], b + ((u // E + 1) // CH + 1))
                if tile_ok and u % E == 2:
                    norm.normalise(dve, x1_sb[tc], tn)

            def softmax():
                dve.wait_ge(S["logits_psum"], 1)
                dve.tensor_tensor(expd[:, :, :], y_ps[:, 0, 0:TB * E].rearrange("p (t e) -> p t e", e=E),
                                  br_sb[:, :].unsqueeze(1).to_broadcast([P, TB, E]), ALU.add) \
                    .then_inc(S["logits_ready"], 1)
                dve.wait_ge(S["logits_ready"], 1)
                dve.tensor_reduce(top[:, :], expd[:, :, :], AX.X, ALU.max).then_inc(S["top_ready"], 1)
                dve.wait_ge(S["top_ready"], 1)
                dve.tensor_tensor(logits[:, :, :], expd[:, :, :], top[:, :].unsqueeze(2).to_broadcast([P, TB, E]),
                                  ALU.subtract).then_inc(S["centred_ready"], 1)
                dve.wait_ge(S["exp_ready"], 1)
                dve.tensor_reduce(total[:, :], expd[:, :, :], AX.X, ALU.add).then_inc(S["total_ready"], 1)
                dve.wait_ge(S["total_ready"], 1)
                dve.reciprocal(inv[:, :], total[:, :]).then_inc(S["inv_ready"], 1)
                dve.wait_ge(S["inv_ready"], 1)
                dve.tensor_tensor(w_sb[:, :, :], expd[:, :, :], inv[:, :].unsqueeze(2).to_broadcast([P, TB, E]),
                                  ALU.mult).then_inc(S["w_ready"], 1)

            split_x(1)
            slot(0, -3, B == 1)
            softmax()
            for i in (0, 1):
                part = slice(i * WP, (i + 1) * WP)
                dve.wait_ge(S["wo_hi_ready"], i + 1)
                dve.tensor_tensor(wo_lo[:, part, :].rearrange("p e c -> p (e c)"), wo_stage[:, i * WL:(i + 1) * WL],
                                  bits(wo_hi[:, part, :]).rearrange("p e c -> p (e c)"), ALU.subtract) \
                    .then_inc(S["wo_lo_ready"], 1)
            slot(0, -2, B == 1)
            slot(0, -1, B == 1)
            if B > 1:
                with dve.Fori(0, B - 1) as b:
                    for u in range(US):
                        slot(b, u, False)
            for u in range(US):
                slot(B - 1, u, True)


def n_par(t):
    return t % 2


INPUTS = ["x", "adj", "L0_gnn_W", "L0_gnn_a", "L0_ffn_Wr", "L0_ffn_br",
          "L0_ffn_W1", "L0_ffn_b1", "L0_ffn_g1", "L0_ffn_be1", "L0_ffn_m1", "L0_ffn_v1",
          "L0_ffn_W2", "L0_ffn_b2", "L0_ffn_g2", "L0_ffn_be2", "L0_ffn_m2", "L0_ffn_v2", "L0_ffn_Wo", "L0_ffn_bo"]


def kernel(**inputs):
    import numpy as np
    import concourse.bacc as bacc
    from concourse.bass_utils import run_bass_kernel_spmd

    nc = bacc.Bacc("TRN2", target_bir_lowering=False, num_devices=1)
    arrays, args = {}, []
    for name in INPUTS:
        array = np.ascontiguousarray(inputs[name])
        arrays[f"in_{name}"] = array
        args.append(nc.dram_tensor(f"in_{name}", array.shape, mybir.dt.from_np(array.dtype), kind="ExternalInput").ap())
    args.append(nc.dram_tensor("out", arrays["in_x"].shape, FP32, kind="ExternalOutput").ap())
    program(nc, *args)
    result = run_bass_kernel_spmd(nc, [arrays], core_ids=[0])
    return result.results[0]["out"]
```
